# Optimizing a Trainium2 kernel written in Bass

```python
import numpy as np
import jax
import jax.numpy as jnp

def _softmax(x, axis=-1):
    return jax.nn.softmax(x, axis=axis)

def _gelu(x):
    return jax.nn.gelu(x, approximate=True)

def _silu(x):
    return jax.nn.silu(x)

def _sigmoid(x):
    return jax.nn.sigmoid(x)

def _layernorm(x, axis=-1, eps=1e-05):
    m = jnp.mean(x, axis=axis, keepdims=True)
    v = jnp.var(x, axis=axis, keepdims=True)
    return (x - m) / jnp.sqrt(v + eps)

def _scatter_add(tgt, idx, src, axis=0):
    return tgt.at[idx].add(src)

def _segment_sum(src, seg, n):
    return jax.ops.segment_sum(src, seg, n)
kernel_name = 'mk_gnn_resnorm_d1_gnn_r8_741484'

def setup_inputs(seed: int=0):
    np.random.seed(seed)
    _w = jnp.asarray

    def _rec_inputs():
        import jax
        import jax.numpy as jnp
        _gk = jax.random.key(seed)
        x = -0.000364 + 1 * jax.random.normal(jax.random.fold_in(_gk, 1), (1250, 768), jnp.float32)
        _s = jax.random.randint(jax.random.fold_in(_gk, 2), (10000,), 0, 1250, jnp.int32)
        _d = jax.random.randint(jax.random.fold_in(_gk, 3), (10000,), 0, 1250, jnp.int32)
        _loop = jnp.arange(1250, dtype=jnp.int32)
        src = jnp.concatenate([_s, _d, _loop])
        dst = jnp.concatenate([_d, _s, _loop])
        _o = jnp.argsort(dst, stable=True)
        src = src[_o]
        dst = dst[_o]
        edge_type_8 = jax.random.randint(jax.random.fold_in(_gk, 12), (21250,), 0, 8, jnp.int32)
        return (x, src, dst, edge_type_8)
    x, src, dst, edge_type_8 = _rec_inputs()

    def _L0_gnn_setup():
        import jax, jax.numpy as jnp
        import numpy as np
        N, IN, OUT, R, E = (2500, 768, 768, 8, 40000)

        def _rgcn_conv(x, src, dst, etype, W, root, b):
            num_nodes = x.shape[0]
            num_rel = W.shape[0]
            x_src = x[src]
            seg = dst * num_rel + etype
            sums = jax.ops.segment_sum(x_src, seg, num_segments=num_nodes * num_rel)
            cnt = jax.ops.segment_sum(jnp.ones((src.shape[0],), dtype=x.dtype), seg, num_segments=num_nodes * num_rel)
            mean = sums / jnp.maximum(cnt, 1.0)[:, None]
            mean = mean.reshape(num_nodes, num_rel, -1)
            out = jnp.einsum('nri,rio->no', mean, W)
            return out + x @ root + b
        key = jax.random.key(seed)
        ks = jax.random.split(key, 9)
        x = jax.random.normal(ks[0], (N, IN), dtype=jnp.float32)
        edge_index = jax.random.randint(ks[1], (2, E), 0, N, dtype=jnp.int64)
        edge_type = jax.random.randint(ks[2], (E,), 0, R, dtype=jnp.int64)
        s1 = 1.0 / np.sqrt(IN)
        s2 = 1.0 / np.sqrt(OUT)
        W1 = jax.random.normal(ks[3], (R, IN, OUT), dtype=jnp.float32) * s1
        root1 = jax.random.normal(ks[4], (IN, OUT), dtype=jnp.float32) * s1
        b1 = jnp.zeros((OUT,), dtype=jnp.float32)
        W2 = jax.random.normal(ks[5], (R, OUT, OUT), dtype=jnp.float32) * s2
        root2 = jax.random.normal(ks[6], (OUT, OUT), dtype=jnp.float32) * s2
        b2 = jnp.zeros((OUT,), dtype=jnp.float32)
        return {'x': x, 'edge_index': edge_index, 'edge_type': edge_type, 'W1': W1, 'root1': root1, 'b1': b1, 'W2': W2, 'root2': root2, 'b2': b2}
    _L0_gnn_all = _L0_gnn_setup()
    _L0_gnn_in = {k: v for k, v in _L0_gnn_all.items() if k in ('W1', 'root1', 'b1', 'W2', 'root2', 'b2')}
    del _L0_gnn_all
    return {'x': x, 'src': src, 'dst': dst, 'edge_type_8': edge_type_8, 'L0_gnn_W1': _L0_gnn_in['W1'], 'L0_gnn_root1': _L0_gnn_in['root1'], 'L0_gnn_b1': _L0_gnn_in['b1'], 'L0_gnn_W2': _L0_gnn_in['W2'], 'L0_gnn_root2': _L0_gnn_in['root2'], 'L0_gnn_b2': _L0_gnn_in['b2']}

def reference(x, src, dst, edge_type_8, L0_gnn_W1, L0_gnn_root1, L0_gnn_b1, L0_gnn_W2, L0_gnn_root2, L0_gnn_b2):
    import jax
    import jax.numpy as jnp

    def _L0_gnn_ref(x, edge_index, edge_type, W1, root1, b1, W2, root2, b2):
        import jax, jax.numpy as jnp
        import numpy as np
        N, IN, OUT, R, E = (2500, 768, 768, 8, 40000)

        def _rgcn_conv(x, src, dst, etype, W, root, b):
            num_nodes = x.shape[0]
            num_rel = W.shape[0]
            x_src = x[src]
            seg = dst * num_rel + etype
            sums = jax.ops.segment_sum(x_src, seg, num_segments=num_nodes * num_rel)
            cnt = jax.ops.segment_sum(jnp.ones((src.shape[0],), dtype=x.dtype), seg, num_segments=num_nodes * num_rel)
            mean = sums / jnp.maximum(cnt, 1.0)[:, None]
            mean = mean.reshape(num_nodes, num_rel, -1)
            out = jnp.einsum('nri,rio->no', mean, W)
            return out + x @ root + b
        src, dst = (edge_index[0], edge_index[1])
        h = _rgcn_conv(x, src, dst, edge_type, W1, root1, b1)
        h = jax.nn.relu(h)
        out = _rgcn_conv(h, src, dst, edge_type, W2, root2, b2)
        return out
    edge_index = jnp.stack([src, dst])
    x = _layernorm(x + _L0_gnn_ref(x, edge_index, edge_type_8, L0_gnn_W1, L0_gnn_root1, L0_gnn_b1, L0_gnn_W2, L0_gnn_root2, L0_gnn_b2), axis=-1)
    return x

_drawn_inputs = setup_inputs


def setup_inputs(seed=0):
    import zlib

    import numpy as np

    out = dict(_drawn_inputs(seed))
    spreads = {'L0_gnn_b1': (0.0, 0.1), 'L0_gnn_b2': (0.0, 0.303)}
    factors = {}
    for name, (base, spread) in spreads.items():
        noise = np.random.default_rng([zlib.crc32(name.encode()), seed]).standard_normal(out[name].shape)
        drawn = base * np.exp(spread * noise) if base else spread * noise
        out[name] = jnp.asarray(drawn.astype(out[name].dtype))
    for name, factor in factors.items():
        out[name] = (out[name] * factor).astype(out[name].dtype)
    return out
```

```python
import math
from contextlib import ExitStack

import concourse.bass as bass
from concourse import mybir


def rgcn_residual_layernorm(nc, x, src, dst, etype, w_all, b1, b2, out):
    f32, f32r, bf16, i32 = mybir.dt.float32, mybir.dt.float32r, mybir.dt.bfloat16, mybir.dt.int32
    ALU, ACT, AX = mybir.AluOpType, mybir.ActivationFunctionType, mybir.AxisListType

    N, D = x.shape
    E = src.shape[0]
    Q = w_all.shape[0]
    R = Q // 2 - 1
    P = 128
    K = D // P
    HALF = D // 2
    T = -(-N // P)
    ROWS = [min(P, N - t * P) for t in range(T)]
    LOG_P = P.bit_length() - 1
    EP = max(p for p in range(1, P + 1) if E % p == 0)
    EJ = E // EP
    NB = R * T
    SEG = 2 * T

    def bucket_tiles(t):
        mean = ROWS[t] * E / N / R
        return math.ceil((mean + 3 * math.sqrt(mean)) / P)

    BT = bucket_tiles(0)
    BT_LAST = bucket_tiles(T - 1)
    assert all(bucket_tiles(t) == BT for t in range(T - 1)) and BT_LAST <= BT
    RT = BT * (T - 1) + BT_LAST
    MAIN = R * RT
    SPILL = -(-E // P)
    COLS = MAIN + SPILL
    FIRST = [BT * t for t in range(T)]
    END = FIRST[1:] + [RT]
    SLOT = [i % BT for i in range(RT)]
    NSPLIT = BT
    NRAW = 6
    RAW_USES = [len(range(s, RT, NRAW)) for s in range(NRAW)]
    IDX_CUT = (RT + 1) // 2
    STEPS = 2 * T
    BANKS = 4
    CJ = 10
    CHUNKS = EJ // CJ
    ROOT1 = R // 2
    ROOT2 = R + 1
    NEAR = 5
    EPS = 1e-5
    assert T % 2 == 0 and STEPS % BANKS == 0 and EJ % CJ == 0 and CHUNKS <= STEPS and R == 8 and T == 10

    ctx = ExitStack()
    with ctx:
        def sb(name, shape, dt=f32):
            return ctx.enter_context(nc.sbuf_tensor(name, shape, dt))

        def sem(name):
            return ctx.enter_context(nc.semaphore(name))

        y = nc.dram_tensor("y", (R * N, D), f32).ap()
        table = nc.dram_tensor("edge_table", (P * COLS, 2), i32).ap()

        h_high = sb("h_high", [P, K, T * P], f32r)
        h_low = sb("h_low", [P, K, T * P], f32r)
        w_high = sb("w_high", [P, 2, K, HALF], f32r)
        w_low = sb("w_low", [P, 2, K, HALF], f32r)
        w_raw = sb("w_raw", [P, K, HALF])
        y_stage = sb("y_stage", [P, BANKS, HALF])
        one_hot = sb("one_hot", [P, 2, BT, P], f32r)
        bias = sb("bias", [P, 2, D])
        edges = sb("edges", [P, COLS, 2], i32)
        dst_local = sb("dst_local", [P, R, BT * T])
        bucket_gid = sb("bucket_gid", [P, R, BT * T], i32)
        bucket_base = sb("bucket_base", [P, R, BT * T])
        inv_count = sb("inv_count", [P, NB])
        index_a = sb("index_a", [P, IDX_CUT], i32)
        index_b = sb("index_b", [P, RT - IDX_CUT], i32)
        identity = sb("identity", [P, P])
        column = sb("column", [P, P], bf16)
        column_i = sb("column_i", [P, P], i32)
        before = sb("before", [P, P], bf16)
        ones = sb("ones", [P, P], bf16)
        eps = sb("eps", [P, 1])
        stats = sb("stats", [P, 2, 2, 6])
        moments = sb("moments", [P, 2, 2])
        std = sb("std", [P, 2, 2])
        spill_n = sb("spill_n", [P, 1], i32)
        spill_index = sb("spill_index", [P, 1], i32)
        spill_gid = sb("spill_gid", [P, 1])
        payload = sb("payload", [EP, EJ, 2], i32)
        position = sb("position", [EP, EJ], i32)
        dl_bf = sb("dl_bf", [EP, EJ], bf16)
        key_bf = sb("key_bf", [EP, EJ], bf16)
        small = sb("small", [P, 4, NB])
        small_bf = sb("small_bf", [P, 3, NB], bf16)
        edge_i = sb("edge_i", [EP, 4, EJ], i32)
        top = nc.sbuf_base if isinstance(nc.sbuf_base, int) else nc.sbuf_base()
        region = sb("region", [P, (T + NRAW + 2 * NSPLIT + 2) * D])
        base = -(-top // 32) * 32

        def at(name, shape, dt, offset):
            return nc.alloc_sbuf_tensor_at(name, shape, dt, offset=base + offset * 4)

        A0, G0, X0 = 0, T * D, (T + NRAW + 2 * NSPLIT) * D
        acc = at("acc", [P, T, D], f32, A0)
        raw = at("raw", [P, NRAW, D], f32, G0)
        g_high = at("g_high", [P, NSPLIT, D], f32r, G0 + NRAW * D)
        g_low = at("g_low", [P, NSPLIT, D], f32r, G0 + (NRAW + NSPLIT) * D)
        x_rows = at("x_rows", [P, 2, D], f32, X0)
        is_key = at("is_key", [EP, NB, EJ], bf16, G0)
        assert NB * EJ * 2 <= (NRAW + 2 * NSPLIT) * D * 4
        ranks = at("ranks", [EP, SEG, EJ], f32, A0)
        go_on = at("go_on", [EP, SEG, EJ], bf16, A0 + SEG * EJ)
        EF = A0 + -(-SEG * EJ * 3 // 16) * 8
        edge_f = at("edge_f", [EP, 12, EJ], f32, EF)
        assert EF + 12 * EJ <= T * D
        dst_hot = at("dst_hot", [EP, 2, CJ, P], bf16, X0)
        assert 2 * CJ * P * 2 <= 2 * D * 4

        prod = ctx.enter_context(nc.psum_tensor("prod", [P, BANKS, 512], f32))
        agg = ctx.enter_context(nc.psum_tensor("agg", [P, 2, 2, 512], f32))

        consts_set = sem("consts_set")
        keys_loaded = sem("keys_loaded")
        x_loaded = [sem(f"x_loaded{s}") for s in range(2)]
        bias_loaded = sem("bias_loaded")
        table_cleared = sem("table_cleared")
        dve_step = sem("dve_step")
        pool_step = sem("pool_step")
        rows_counted = sem("rows_counted")
        rows_summed = sem("rows_summed")
        flags_counted = sem("flags_counted")
        flags_summed = sem("flags_summed")
        positions_ready = sem("positions_ready")
        scattered = sem("scattered")
        table_loaded = sem("table_loaded")
        index_loaded = sem("index_loaded")
        hot_ready = sem("hot_ready")
        chunk_counted = sem("chunk_counted")
        transposed = sem("transposed")
        h_high_ready = sem("h_high_ready")
        h_low_ready = sem("h_low_ready")
        w_loaded = sem("w_loaded")
        w_high_ready = sem("w_high_ready")
        w_low_ready = sem("w_low_ready")
        prod_done = sem("prod_done")
        y_staged = sem("y_staged")
        y_stored = [sem(f"y_stored{s}") for s in range(BANKS)]
        root_kept = sem("root_kept")
        raw_loaded = [sem(f"raw_loaded{s}") for s in range(NRAW)]
        high_ready = sem("high_ready")
        low_ready = sem("low_ready")
        one_hot_ready = sem("one_hot_ready")
        tile_used = sem("tile_used")
        bucket_added = sem("bucket_added")
        residual_loaded = [sem(f"residual_loaded{s}") for s in range(2)]
        x_biased = sem("x_biased")
        residual_added = sem("residual_added")
        var_ready = sem("var_ready")
        std_ready = sem("std_ready")
        normed = sem("normed")
        out_stored = sem("out_stored")
        spill_copied = [sem(f"spill_copied{l}") for l in range(2)]
        spill_shifted = [sem(f"spill_shifted{l}") for l in range(2)]
        spill_loaded = [sem(f"spill_loaded{l}") for l in range(2)]
        spill_high = [sem(f"spill_high{l}") for l in range(2)]
        spill_low = [sem(f"spill_low{l}") for l in range(2)]
        spill_hot = [sem(f"spill_hot{l}") for l in range(2)]
        spill_summed = [sem(f"spill_summed{l}") for l in range(2)]
        spill_added = [sem(f"spill_added{l}") for l in range(2)]

        def unit(q, h):
            return 2 * q + h

        def lagging(s):
            return [t for t in range(T) if s == min(2 * t + 3, STEPS - 1)]

        block = ctx.enter_context(nc.Block())

        @block.sync
        def _(sp):
            def load_unit(q, h):
                u = unit(q, h)
                if not (isinstance(q, int) and u == 0):
                    sp.wait_ge(w_high_ready, u)
                    sp.wait_ge(w_low_ready, u)
                w = w_all[bass.ds(q, 1), :, h * HALF:(h + 1) * HALF].rearrange("o (k p) n -> p (o k) n", p=P)
                sp.dma_start(w_raw[:], w).then_inc(w_loaded, 16)

            def store_y(layer, r, s):
                h, t = divmod(s, T)
                sp.wait_ge(y_staged, STEPS * (layer * R + r) + s + 1)
                sp.dma_start(y[bass.ds(r * N + t * P, ROWS[t]), h * HALF:(h + 1) * HALF],
                             y_stage[0:ROWS[t], s % BANKS, :]).then_inc(y_stored[s % BANKS], 16)

            def relation(q, layer, r, more=True):
                for s in range(STEPS):
                    store_y(layer, r, s)
                    if more and s == 4:
                        load_unit(q + 1, 0)
                    if more and s == 14:
                        load_unit(q + 1, 1)

            for n, a in enumerate((dst, etype, src)):
                sp.dma_start(edge_i[:, n, :], a.rearrange("(p j) -> p j", p=EP)).then_inc(keys_loaded, 16)
            load_unit(0, 0)
            for t in range(T):
                if t >= 2:
                    sp.wait_ge(transposed, 2 * (t - 1))
                sp.dma_start(x_rows[0:ROWS[t], t % 2, :],
                             x[t * P:t * P + ROWS[t], :]).then_inc(x_loaded[t % 2], 16)
            load_unit(0, 1)
            for n, b in enumerate((b1, b2)):
                sp.dma_start(bias[:, n, :], b.rearrange("(o n) -> o n", o=1).to_broadcast([P, D]))\
                    .then_inc(bias_loaded, 16)
            sp.wait_ge(consts_set, 1)
            sp.dma_start(table.rearrange("(p c) w -> p (c w)", p=P),
                         edges[:].rearrange("p c w -> p (c w)")).then_inc(table_cleared, 16)

            with sp.Fori(0, ROOT1) as r:
                relation(r, 0, r)
            load_unit(ROOT1 + 1, 0)
            sp.wait_ge(scattered, 16 * EJ)
            sp.dma_start(edges[:].rearrange("p c w -> p (c w)"),
                         table.rearrange("(p c) w -> p (c w)", p=P)).then_inc(table_loaded, 16)
            load_unit(ROOT1 + 1, 1)
            with sp.Fori(ROOT1, R) as r:
                relation(r + 1, 0, r)
            load_unit(ROOT2 + 1, 0)
            load_unit(ROOT2 + 1, 1)

            sp.wait_ge(chunk_counted, CHUNKS)
            for t in range(T):
                if t >= 2:
                    sp.wait_ge(residual_added, t - 1)
                sp.dma_start(x_rows[0:ROWS[t], t % 2, :],
                             x[t * P:t * P + ROWS[t], :]).then_inc(residual_loaded[t % 2], 16)
                for s in (2 * t, 2 * t + 1):
                    store_y(1, 0, s)
                    if s == 4:
                        load_unit(ROOT2 + 2, 0)
                    if s == 14:
                        load_unit(ROOT2 + 2, 1)
            with sp.Fori(1, R - 1) as r:
                relation(r + ROOT2 + 1, 1, r)
            relation(R + ROOT2, 1, R - 1, more=False)
            for t in range(T):
                sp.wait_ge(normed, t + 1)
                sp.dma_start(out[t * P:t * P + ROWS[t], :], acc[0:ROWS[t], t, :]).then_inc(out_stored, 16)
            sp.wait_ge(out_stored, 16 * T)

        @block.gpsimd
        def _(pool):
            steps = [0]

            def link(ins):
                steps[0] += 1
                ins.then_inc(pool_step, 1)
                pool.wait_ge(pool_step, steps[0])

            pool.memset(edges[:, :, 0], R * N)
            link(pool.memset(edges[:, :, 1], -1))
            pool.memset(before[:], 1.0)
            pool.memset(ones[:], 1.0)
            pool.memset(eps[:], EPS)
            pool.iota(column_i[:], [[1, P]], base=0, channel_multiplier=0)
            pool.iota(bucket_gid[:].rearrange("p r (t b) -> p r t b", b=BT),
                      [[T * P, R], [P, T], [0, BT]], base=0, channel_multiplier=0)
            link(pool.memset(identity[:], 0.0))
            pool.affine_select(out=identity[:], in_=identity[:], compare_op=ALU.not_equal, fill=1.0, base=0,
                               pattern=[[-1, P]], channel_multiplier=1)
            link(pool.affine_select(out=before[:], in_=before[:], compare_op=ALU.is_gt, fill=0.0, base=0,
                                    pattern=[[1, P]], channel_multiplier=-1))
            pool.nop().then_inc(consts_set, 1)
            row_limit = pool.to_reg(R * N - 1)

            def low_of_unit(q, h):
                u = unit(q, h)
                pool.wait_ge(w_high_ready, u + 1)
                pool.tensor_tensor(w_low[:, h], w_raw[:], w_high[:, h].bitcast(f32), ALU.subtract)\
                    .then_inc(w_low_ready, 1)

            def wait_both(semaphore, value):
                value = value if isinstance(value, int) else pool.snap(pool.to_reg(value))
                pool.wait_ge(table_loaded, 16)
                pool.wait_ge(semaphore, value)

            def load_index(part, r, count):
                buf, first = ((index_a, 0), (index_b, IDX_CUT))[part]
                n = buf.shape[1]
                pool.tensor_copy(buf[:], edges[:, bass.ds(r * RT + first, n), 0]).then_inc(index_loaded, 1)
                wait_both(index_loaded, count)

            def gather(g, r, i, written, last=False):
                slot = i % NRAW
                if i == 0:
                    for s in range(BANKS):
                        pool.wait_ge(y_stored[s], 16 * (STEPS // BANKS) * (g + 1))
                prev = i - NRAW if i >= NRAW else max(range(slot, RT, NRAW)) - RT
                if last and i >= NRAW:
                    wait_both(tile_used, NSPLIT + RT * g + prev + 1)
                else:
                    wait_both(low_ready, NRAW + RT * g + prev + 1)
                if i == NRAW + 1:
                    load_index(1, r, 2 * g + 2)
                if i == IDX_CUT + NRAW + 1 and not last:
                    load_index(0, 0 if isinstance(r, int) and r == R - 1 else r + 1, 2 * g + 3)
                col = index_a[:, i:i + 1] if i < IDX_CUT else index_b[:, i - IDX_CUT:i - IDX_CUT + 1]
                pool.indirect_dma_start(raw[:, slot, :], None, y[0:written * N, :],
                                        bass.IndirectOffsetOnAxis(ap=col, axis=0),
                                        bounds_check=row_limit, oob_is_err=False)\
                    .then_inc(raw_loaded[slot], 16)

            def gather_relation(g, r, written=R, last=False):
                for t in range(T):
                    for i in range(FIRST[t], END[t]):
                        gather(g, r, i, written, last)

            def gather_spilled(layer, g):
                for s in range(BANKS):
                    pool.wait_ge(y_stored[s], 16 * (STEPS // BANKS) * (g + 1))
                pool.wait_ge(low_ready, NRAW + RT * g)
                n = pool.value_load(spill_n[0:1, 0:1], min_val=0, max_val=SPILL)
                with pool.If(n > 0):
                    with pool.Fori(0, n) as i:
                        pool.wait_ge(spill_added[layer], NB * i + 1)
                        pool.tensor_copy(spill_index[:], edges[:, bass.ds(i + MAIN, 1), 0])\
                            .then_inc(spill_copied[layer], 1)
                        wait_both(spill_copied[layer], i + 1)
                        pool.indirect_dma_start(raw[:, 0, :], None, y,
                                                bass.IndirectOffsetOnAxis(ap=spill_index[:], axis=0),
                                                bounds_check=row_limit, oob_is_err=False)\
                            .then_inc(spill_loaded[layer], 16)
                    pool.wait_ge(spill_added[layer], NB * n + 1)
                pool.end_ifs()

            for u in range(NEAR):
                low_of_unit(u // 2, u % 2)
            pool.wait_ge(table_cleared, 16)
            pool.wait_ge(positions_ready, 1)
            for j in range(EJ):
                pool.indirect_dma_start(table, bass.IndirectOffsetOnAxis(ap=position[:, j:j + 1], axis=0),
                                        payload[:, j, :], None).then_inc(scattered, 16)
            pool.wait_ge(scattered, 16 * EJ)
            pool.wait_ge(chunk_counted, CHUNKS)
            link(pool.memset(raw[:], 0.0))
            pool.wait_ge(table_loaded, 16)
            load_index(0, 0, 1)

            for s in range(BANKS):
                pool.wait_ge(y_stored[s], 16 * (STEPS // BANKS) * ROOT1)
            with pool.Fori(0, ROOT1) as r:
                gather_relation(r, r, ROOT1)
            for r in range(ROOT1, R - 1):
                gather_relation(r, r, r + 1)
            gather_spilled(0, R - 1)
            gather_relation(R - 1, R - 1)

            for t in range(T):
                pool.wait_ge(residual_loaded[t % 2], 16 * (t // 2 + 1))
                pool.wait_ge(bias_loaded, 32)
                pool.tensor_tensor(x_rows[:, t % 2, :], x_rows[:, t % 2, :], bias[:, 1, :], ALU.add)\
                    .then_inc(x_biased, 1)
            with pool.Fori(0, R - 1) as r:
                gather_relation(r + R, r)
            gather_spilled(1, 2 * R - 1)
            gather_relation(2 * R - 1, R - 1, last=True)

        @block.scalar
        def _(act):
            def high_of_unit(q, h):
                u = unit(q, h)
                act.wait_ge(w_loaded, 16 * (u + 1))
                if not (isinstance(q, int) and q == 0):
                    act.wait_ge(prod_done, T * (u - 1))
                act.activation(w_high[:, h], w_raw[:], ACT.Copy).then_inc(w_high_ready, 1)

            def high_of_tile(g, i):
                slot = i % NRAW
                act.wait_ge(raw_loaded[slot], 16 * (RAW_USES[slot] * g + i // NRAW + 1))
                prev = i - NSPLIT if i >= NSPLIT else max(range(SLOT[i], RT, NSPLIT)) - RT
                act.wait_ge(tile_used, NSPLIT + RT * g + prev + 1)
                act.activation(g_high[:, SLOT[i], :], raw[:, slot, :], ACT.Copy).then_inc(high_ready, 1)

            def bucket(g, t):
                for i in range(FIRST[t], END[t]):
                    high_of_tile(g, i)

            def stage_y(g, k, s):
                act.wait_ge(prod_done, k + 1)
                if not (isinstance(g, int) and g == 0 and s < BANKS):
                    act.wait_ge(y_stored[s % BANKS], 16 * ((STEPS // BANKS) * g + s // BANKS))
                act.activation(y_stage[:, s % BANKS, :], prod[:, s % BANKS, 0:HALF], ACT.Copy)\
                    .then_inc(y_staged, 1)

            def relation(q, g, summed=None, more=True, first_split=True):
                for s in range(STEPS):
                    for b in summed(s) if summed else ():
                        bucket(*b)
                    stage_y(g, STEPS * q + s, s)
                    if s == 1 and first_split:
                        high_of_unit(q, 1)
                    if s == 11 and more:
                        high_of_unit(q + 1, 0)

            def high_spilled(layer, g):
                act.wait_ge(positions_ready, 1)
                act.wait_ge(tile_used, NSPLIT + RT * g)
                n = act.value_load(spill_n[0:1, 0:1], min_val=0, max_val=SPILL)
                with act.If(n > 0):
                    with act.Fori(0, n) as i:
                        act.wait_ge(spill_loaded[layer], i * 16 + 16)
                        act.activation(g_high[:, 0, :], raw[:, 0, :], ACT.Copy).then_inc(spill_high[layer], 1)
                act.end_ifs()

            high_of_unit(0, 0)
            for u in range(2 * T):
                act.wait_ge(transposed, u + 1)
                act.activation(h_high[:, 3 * (u % 2):3 * (u % 2) + 3, (u // 2) * P:(u // 2 + 1) * P],
                               prod[:, u % BANKS, 0:HALF].rearrange("p (k n) -> p k n", n=P), ACT.Copy)\
                    .then_inc(h_high_ready, 1)
            relation(0, 0)
            with act.Fori(1, ROOT1) as r:
                relation(r, r)
            high_of_unit(ROOT1, 1)
            high_of_unit(ROOT1 + 1, 0)
            with act.Fori(ROOT1, R - 1) as r:
                relation(r + 1, r, summed=lambda s: [(2 * r - 2 * ROOT1 + s // T, s % T)])
            relation(R, R - 1, summed=lambda s: [(R - 2, t) for t in lagging(s)])
            high_spilled(0, R - 1)
            high_of_unit(ROOT2, 1)
            bucket(R - 1, 0)
            for t in range(T):
                if t + 1 < T:
                    bucket(R - 1, t + 1)
                for hh in range(2):
                    u = 2 * T + 2 * t + hh
                    act.wait_ge(transposed, u + 1)
                    act.activation(h_high[:, 3 * hh:3 * hh + 3, t * P:(t + 1) * P],
                                   prod[:, hh, 0:HALF].rearrange("p (k n) -> p k n", n=P), ACT.Relu)\
                        .then_inc(h_high_ready, 1)
            high_of_unit(ROOT2 + 1, 0)
            relation(ROOT2 + 1, R)
            with act.Fori(1, R - 1) as r:
                relation(r + ROOT2 + 1, r + R, summed=lambda s: [(r + R - 1, t) for t in lagging(s)])
            relation(R + ROOT2, 2 * R - 1, summed=lambda s: [(2 * R - 2, t) for t in lagging(s)], more=False)
            high_spilled(1, 2 * R - 1)
            for t in range(T):
                act.wait_ge(var_ready, t + 1)
                act.activation(std[:, t % 2, 0:1], moments[:, t % 2, 1:2], ACT.Sqrt, bias=eps[:])\
                    .then_inc(std_ready, 1)

        @block.tensor
        def _(pe):
            def transpose_half(read, u, bank):
                for k in range(3):
                    c = 3 * (u % 2) + k
                    mm = pe.transpose(prod[:, bank, k * P:(k + 1) * P], read[:, c * P:(c + 1) * P], identity[:])
                mm.then_inc(transposed, 1)

            def product(q, h, t, bank):
                n = K * 3
                for k in range(K):
                    for left, right in ((h_high, w_high), (h_high, w_low), (h_low, w_high)):
                        n -= 1
                        mm = pe.matmul(prod[:, bank, 0:HALF], left[:, k, t * P:(t + 1) * P], right[:, h, k, :],
                                       start=(k == 0 and left is h_high and right is w_high), stop=(n == 0))
                return mm

            def unit_ready(q, h):
                pe.wait_ge(w_high_ready, unit(q, h) + 1)
                pe.wait_ge(w_low_ready, unit(q, h) + 1)

            def step(q, s, free):
                h, t = divmod(s, T)
                if t == 0:
                    unit_ready(q, h)
                if free is not None:
                    pe.wait_ge(*free)
                product(q, h, t, s % BANKS).then_inc(prod_done, 1)

            def bucket(g, t):
                par = t % 2
                pe.wait_ge(bucket_added, T * g + t + 1)
                pe.wait_ge(one_hot_ready, T * g + t + 1)
                last = END[t] - 1
                for i in range(FIRST[t], END[t]):
                    pe.wait_ge(low_ready, NRAW + RT * g + i + 1)
                    for part in (g_high, g_low):
                        for c in range(2):
                            mm = pe.matmul(agg[:, par, c, 0:HALF], one_hot[:, par, i - FIRST[t], :],
                                           part[:, SLOT[i], c * HALF:(c + 1) * HALF],
                                           start=(i == FIRST[t] and part is g_high),
                                           stop=(i == last and part is g_low), skip_group_check=True)
                    mm.then_inc(tile_used, 1)

            def sum_rows():
                pe.wait_ge(rows_counted, 1)
                pe.matmul(agg[:, 1, 0, 0:NB], before[0:EP, :], small_bf[0:EP, 1, :], start=True, stop=True)\
                    .then_inc(rows_summed, 1)

            def sum_flags():
                pe.wait_ge(flags_counted, 1)
                pe.matmul(agg[:, 1, 0, 0:1], before[0:EP, :], small_bf[0:EP, 2, 0:1], start=True, stop=True)
                pe.matmul(agg[:, 1, 1, 0:1], ones[0:EP, :], small_bf[0:EP, 2, 0:1], start=True, stop=True)\
                    .then_inc(flags_summed, 1)

            def sum_spilled(layer, g):
                pe.wait_ge(positions_ready, 1)
                pe.wait_ge(bucket_added, 2 + T * g)
                n = pe.value_load(spill_n[0:1, 0:1], min_val=0, max_val=SPILL)
                with pe.If(n > 0):
                    with pe.Fori(0, n) as i:
                        with pe.Fori(0, R) as r:
                            for t in range(T):
                                pe.wait_ge(spill_low[layer], i + 1)
                                pe.wait_ge(spill_hot[layer], i * NB + r * T + t + 1)
                                for part in (g_high, g_low):
                                    for c in range(2):
                                        mm = pe.matmul(agg[:, 0, c, 0:HALF], one_hot[:, 0, 0, :],
                                                       part[:, 0, c * HALF:(c + 1) * HALF],
                                                       start=part is g_high, stop=part is g_low,
                                                       skip_group_check=True)
                                mm.then_inc(spill_summed[layer], 1)
                pe.end_ifs()

            def relation(q, g, summed=None, middle=None):
                for s in range(STEPS):
                    if s == T and middle:
                        middle()
                    first = isinstance(g, int) and g == 0 and s < BANKS
                    step(q, s, None if first else (y_staged, STEPS * g + s - BANKS + 1))
                    for b in summed(s) if summed else ():
                        bucket(*b)

            pe.wait_ge(pool_step, 3)
            pe.wait_ge(consts_set, 1)
            for u in range(2 * T):
                t = u // 2
                if u % 2 == 0:
                    pe.wait_ge(x_loaded[t % 2], 16 * (t // 2 + 1))
                if u >= BANKS:
                    pe.wait_ge(h_low_ready, u - BANKS + 1)
                transpose_half(x_rows[:, t % 2, :], u, u % BANKS)
            pe.nop().then_inc(tile_used, NSPLIT)
            pe.wait_ge(h_low_ready, 2 * T)
            relation(0, 0, middle=sum_rows)
            relation(1, 1, middle=sum_flags)
            with pe.Fori(2, ROOT1) as r:
                relation(r, r)
            for s in range(STEPS):
                step(ROOT1, s, (y_staged, STEPS * ROOT1 - BANKS + s + 1) if s < BANKS
                     else (root_kept, s - BANKS + 1))
                if s < CHUNKS:
                    pe.wait_ge(hot_ready, s + 1)
                    for j in range(CJ):
                        e = s * CJ + j
                        mm = pe.matmul(agg[:, 0, 0, 0:NB], dst_hot[:, s % 2, j, :], is_key[:, :, e],
                                       start=(e == 0), stop=(e == EJ - 1))
                    mm.then_inc(chunk_counted, 1)
            pe.wait_ge(root_kept, STEPS)
            with pe.Fori(ROOT1, R - 1) as r:
                relation(r + 1, r, summed=lambda s: [(2 * r - 2 * ROOT1 + s // T, s % T)])
            relation(R, R - 1, summed=lambda s: [(R - 2, t) for t in lagging(s)])
            sum_spilled(0, R - 1)

            def root_half(t):
                pe.wait_ge(h_low_ready, 2 * T + 2 * t + 2)
                if t >= 2:
                    pe.wait_ge(root_kept, STEPS + t - 1)
                product(ROOT2, 0, t, 2 + t % 2).then_inc(prod_done, 1)

            pe.wait_ge(y_staged, STEPS * R)
            bucket(R - 1, 0)
            for t in range(T):
                if t + 1 < T:
                    bucket(R - 1, t + 1)
                pe.wait_ge(bucket_added, 2 + T * (R - 1) + t + 1)
                for hh in range(2):
                    if t:
                        pe.wait_ge(h_low_ready, 2 * T + 2 * (t - 1) + hh + 1)
                    transpose_half(acc[:, t, :], 2 * T + 2 * t + hh, hh)
                if t == 0:
                    unit_ready(ROOT2, 0)
                else:
                    root_half(t - 1)
            root_half(T - 1)
            pe.wait_ge(root_kept, STEPS + T)
            unit_ready(ROOT2, 1)
            for t in range(T):
                if t >= BANKS:
                    pe.wait_ge(root_kept, STEPS + T + t - BANKS + 1)
                product(ROOT2, 1, t, t % BANKS).then_inc(prod_done, 1)
            pe.wait_ge(root_kept, 2 * STEPS)

            relation(ROOT2 + 1, R)
            with pe.Fori(1, R) as r:
                relation(r + ROOT2 + 1, r + R, summed=lambda s: [(r + R - 1, t) for t in lagging(s)])
            sum_spilled(1, 2 * R - 1)
            g = 2 * R - 1
            for t in range(T):
                pe.wait_ge(bucket_added, T * g + t + 1)
                pe.wait_ge(one_hot_ready, T * g + t + 1)
                for i in range(FIRST[t], END[t]):
                    pe.wait_ge(raw_loaded[i % NRAW], 16 * (RAW_USES[i % NRAW] * g + i // NRAW + 1))
                    for c in range(2):
                        mm = pe.matmul(agg[:, t % 2, c, 0:HALF], one_hot[:, t % 2, i - FIRST[t], :].bitcast(f32),
                                       raw[:, i % NRAW, c * HALF:(c + 1) * HALF],
                                       start=(i == FIRST[t]), stop=(i == END[t] - 1), skip_group_check=True)
                    mm.then_inc(tile_used, 1)

        @block.vector
        def _(dve):
            steps = [0]

            def link(ins):
                steps[0] += 1
                ins.then_inc(dve_step, 1)
                dve.wait_ge(dve_step, steps[0])

            def low_of_unit(u, h=None):
                dve.wait_ge(w_high_ready, u + 1)
                if isinstance(u, int) and u == NEAR:
                    dve.wait_ge(w_low_ready, u)
                h = h if h is not None else u % 2
                dve.tensor_tensor(w_low[:, h], w_raw[:], w_high[:, h].bitcast(f32), ALU.subtract)\
                    .then_inc(w_low_ready, 1)

            def low_of_half(u, t, bank, relu):
                k = 3 * (u % 2)
                psum = prod[:, bank, 0:HALF].rearrange("p (k n) -> p k n", n=P)
                high = h_high[:, k:k + 3, t * P:(t + 1) * P].bitcast(f32)
                low = h_low[:, k:k + 3, t * P:(t + 1) * P]
                dve.wait_ge(h_high_ready, u + 1)
                if relu:
                    ins = dve.scalar_tensor_tensor(low, psum, 0.0, high, ALU.max, ALU.subtract)
                else:
                    ins = dve.tensor_tensor(low, psum, high, ALU.subtract)
                ins.then_inc(h_low_ready, 1)

            def keep_root(k, t, h, bank, plus=None):
                dve.wait_ge(prod_done, k + 1)
                a = acc[:, t, h * HALF:(h + 1) * HALF]
                if plus is None:
                    ins = dve.tensor_copy(a, prod[:, bank, 0:HALF])
                else:
                    ins = dve.tensor_tensor(a, prod[:, bank, 0:HALF], plus[:, h * HALF:(h + 1) * HALF], ALU.add)
                ins.then_inc(root_kept, 1)

            def prepare(g, r, t, split=True):
                par = t % 2
                dve.wait_ge(tile_used, NSPLIT + RT * g + (END[t - 2] if t >= 2 else END[T - 2 + t] - RT))
                for i in range(FIRST[t], END[t]):
                    ins = dve.tensor_scalar(one_hot[:, par, i - FIRST[t], :], column[:],
                                            dst_flat[:, bass.ds(r * BT * T + i, 1)], None, ALU.is_equal)
                ins.then_inc(one_hot_ready, 1)
                for i in range(FIRST[t], END[t]) if split else ():
                    dve.wait_ge(high_ready, RT * g + i + 1)
                    dve.tensor_tensor(g_low[:, SLOT[i], :], raw[:, i % NRAW, :],
                                      g_high[:, SLOT[i], :].bitcast(f32), ALU.subtract).then_inc(low_ready, 1)

            def add(g, r, t):
                dve.wait_ge(tile_used, NSPLIT + RT * g + END[t])
                a = acc[:, t, :].rearrange("p (c n) -> p c n", c=2)
                dve.scalar_tensor_tensor(a, agg[:, t % 2, :, 0:HALF], inv_count[:, bass.ds(r * T + t, 1)], a,
                                         ALU.mult, ALU.add).then_inc(bucket_added, 1)

            def added(g, t):
                dve.wait_ge(bucket_added, 2 + T * g + t + 1)

            def buckets(which, q=None, weights=(), more=True):
                prepare(*which[0])
                for n, b in enumerate(which):
                    if n + 1 < len(which):
                        prepare(*which[n + 1])
                    add(*b)
                    if n in weights[:1]:
                        low_of_unit(unit(q, 1), 1)
                    if n in weights[1:] and more:
                        low_of_unit(unit(q + 1, 0), 0)

            def add_spilled(layer, g):
                dve.wait_ge(tile_used, NSPLIT + RT * g)
                added(g - 1, T - 1)
                n = dve.value_load(spill_n[0:1, 0:1], min_val=0, max_val=SPILL)
                dve.nop().then_inc(spill_added[layer], 1)
                with dve.If(n > 0):
                    with dve.Fori(0, n) as i:
                        dve.tensor_copy(spill_gid[:], edges[:, bass.ds(i + MAIN, 1), 1])\
                            .then_inc(spill_shifted[layer], 1)
                        dve.wait_ge(spill_high[layer], i + 1)
                        dve.tensor_tensor(g_low[:, 0, :], raw[:, 0, :], g_high[:, 0, :].bitcast(f32),
                                          ALU.subtract).then_inc(spill_low[layer], 1)
                        with dve.Fori(0, R) as r:
                            for t in range(T):
                                b = i * NB + r * T + t
                                dve.wait_ge(spill_shifted[layer], i * (NB + 1) + r * T + t + 1)
                                dve.tensor_scalar(one_hot[:, 0, 0, :], column[:], spill_gid[:], None,
                                                  ALU.is_equal).then_inc(spill_hot[layer], 1)
                                dve.wait_ge(spill_hot[layer], b + 1)
                                dve.tensor_scalar(spill_gid[:], spill_gid[:], float(-P), None, ALU.add)\
                                    .then_inc(spill_shifted[layer], 1)
                                dve.wait_ge(spill_summed[layer], b + 1)
                                a = acc[:, t, :].rearrange("p (c n) -> p c n", c=2)
                                dve.scalar_tensor_tensor(a, agg[:, 0, :, 0:HALF],
                                                         inv_count[:, bass.ds(r * T + t, 1)], a,
                                                         ALU.mult, ALU.add).then_inc(spill_added[layer], 1)
                                dve.wait_ge(spill_added[layer], b + 2)
                dve.end_ifs()

            dst_flat = dst_local[:].rearrange("p r i -> p (r i)")

            dve.wait_ge(consts_set, 1)
            link(dve.tensor_copy(column[:], column_i[:]))
            dve.tensor_copy(bucket_base[:], bucket_gid[:])
            dve.memset(go_on[:], 1.0)

            for u in range(2 * T):
                low_of_half(u, u // 2, u % BANKS, relu=False)

            F = [edge_f[:, n, :] for n in range(12)]
            TILE, DL, TYPE, SRC, KEY, ROW, GID, MPOS, CAP, FLAG, RANK, SPOS = F
            INT = [edge_i[:, n, :] for n in range(4)]
            dve.wait_ge(keys_loaded, 48)
            dve.tensor_scalar(INT[3], INT[0], LOG_P, None, ALU.arith_shift_right)
            dve.tensor_scalar(position[:], INT[0], P - 1, None, ALU.bitwise_and)
            dve.tensor_copy(TYPE, INT[1])
            link(dve.tensor_copy(SRC, INT[2]))
            dve.tensor_copy(TILE, INT[3])
            link(dve.tensor_copy(DL, position[:]))
            dve.tensor_copy(dl_bf[:], DL)
            dve.memset(go_on[:, :, 0], 0.0)
            dve.tensor_copy(small_bf[:, 0, :], column[:, 0:NB])
            link(dve.scalar_tensor_tensor(KEY, TYPE, float(T), TILE, ALU.mult, ALU.add))
            link(dve.tensor_copy(key_bf[:], KEY))
            for b in range(0, NB, SEG):
                link(dve.tensor_tensor(is_key[:, b:b + SEG, :], key_bf[:].unsqueeze(1).to_broadcast([EP, SEG, EJ]),
                                       small_bf[0:EP, 0, b:b + SEG].unsqueeze(2).to_broadcast([EP, SEG, EJ]),
                                       ALU.is_equal))
                link(dve.tensor_reduce(small[0:EP, 0, b:b + SEG], is_key[:, b:b + SEG, :], axis=AX.X, op=ALU.add))
            dve.tensor_copy(small_bf[0:EP, 1, :], small[0:EP, 0, :]).then_inc(rows_counted, 1)

            dve.wait_ge(rows_summed, 1)
            link(dve.tensor_scalar(small[0:EP, 1, :], agg[0:EP, 1, 0, 0:NB], -1.0, None, ALU.add))
            for b in range(0, NB, SEG):
                link(dve.tensor_tensor_scan(ranks[:].rearrange("p b j -> p (b j)"),
                                            go_on[:].rearrange("p b j -> p (b j)"),
                                            is_key[:, b:b + SEG, :].rearrange("p b j -> p (b j)"),
                                            0.0, ALU.mult, ALU.add))
                for c in range(SEG):
                    ins = dve.scalar_tensor_tensor(ranks[:, c, :], ranks[:, c, :], small[0:EP, 1, b + c:b + c + 1],
                                                   is_key[:, b + c, :], ALU.add, ALU.mult)
                link(ins)
                link(dve.tensor_reduce(RANK if b == 0 else FLAG, ranks[:].rearrange("p b j -> p j b"),
                                       axis=AX.X, op=ALU.add))
                if b:
                    link(dve.tensor_tensor(RANK, RANK, FLAG, ALU.add))

            dve.tensor_scalar(CAP, TILE, float(T - 1), float(-P * (BT - BT_LAST)), ALU.is_equal, ALU.mult)
            dve.scalar_tensor_tensor(ROW, TYPE, float(N), SRC, ALU.mult, ALU.add)
            dve.scalar_tensor_tensor(GID, KEY, float(P), DL, ALU.mult, ALU.add)
            link(dve.tensor_scalar(MPOS, TYPE, float(RT * P), None, ALU.mult))
            link(dve.scalar_tensor_tensor(MPOS, TILE, float(BT * P), MPOS, ALU.mult, ALU.add))
            dve.tensor_copy(payload[:, :, 0], ROW)
            dve.tensor_copy(payload[:, :, 1], GID)
            link(dve.tensor_tensor(MPOS, MPOS, RANK, ALU.add))
            link(dve.scalar_tensor_tensor(FLAG, RANK, float(-BT * P), CAP, ALU.add, ALU.is_ge))
            link(dve.tensor_tensor_scan(SPOS, FLAG, FLAG, 0.0, ALU.add, ALU.max))
            dve.tensor_copy(small_bf[0:EP, 2, 0:1], SPOS[:, EJ - 1:EJ]).then_inc(flags_counted, 1)
            dve.wait_ge(flags_summed, 1)
            dve.tensor_scalar(small[0:EP, 2, 0:1], agg[0:EP, 1, 0, 0:1], float(MAIN * P - 1), None, ALU.add)
            link(dve.tensor_scalar(small[:, 3, 0:1], agg[:, 1, 1, 0:1], float(P - 1), None, ALU.add))
            link(dve.tensor_copy(spill_n[:], small[:, 3, 0:1]))
            link(dve.tensor_scalar(spill_n[:], spill_n[:], LOG_P, None, ALU.arith_shift_right))
            link(dve.scalar_tensor_tensor(SPOS, SPOS, small[0:EP, 2, 0:1], MPOS, ALU.add, ALU.subtract))
            link(dve.tensor_tensor(SPOS, SPOS, FLAG, ALU.mult))
            link(dve.tensor_tensor(SPOS, SPOS, MPOS, ALU.add))
            link(dve.tensor_copy(INT[3], SPOS))
            dve.tensor_scalar(INT[0], INT[3], P - 1, None, ALU.bitwise_and)
            link(dve.tensor_scalar(INT[1], INT[3], LOG_P, None, ALU.arith_shift_right))
            dve.tensor_copy(TILE, INT[0])
            link(dve.tensor_copy(DL, INT[1]))
            link(dve.scalar_tensor_tensor(SPOS, TILE, float(COLS), DL, ALU.mult, ALU.add))
            link(dve.tensor_copy(position[:], SPOS))
            dve.nop().then_inc(positions_ready, 1)

            for u in range(NEAR, unit(ROOT1, 1)):
                low_of_unit(u)

            dve.wait_ge(transposed, 2 * T)
            dve.wait_ge(bias_loaded, 32)
            for s in range(STEPS):
                if s < CHUNKS:
                    if s >= 2:
                        dve.wait_ge(chunk_counted, s - 1)
                    dve.tensor_tensor(dst_hot[:, s % 2], column[0:EP, :].unsqueeze(1).to_broadcast([EP, CJ, P]),
                                      dl_bf[:, s * CJ:(s + 1) * CJ].unsqueeze(2).to_broadcast([EP, CJ, P]),
                                      ALU.is_equal).then_inc(hot_ready, 1)
                keep_root(STEPS * ROOT1 + s, s % T, s // T, s % BANKS, plus=bias[:, 0, :])
                if s == 2:
                    low_of_unit(unit(ROOT1, 1))
                if s == 12:
                    low_of_unit(unit(ROOT1 + 1, 0))
            dve.wait_ge(chunk_counted, CHUNKS)
            link(dve.tensor_scalar(inv_count[:], agg[:, 0, 0, 0:NB], 1.0, None, ALU.max))
            link(dve.reciprocal(inv_count[:], inv_count[:]))
            dve.nop().then_inc(bucket_added, 2)
            dve.nop().then_inc(low_ready, NRAW)
            dve.wait_ge(table_loaded, 16)
            used = dst_local[:, :, 0:RT]
            link(dve.tensor_copy(used, edges[:, 0:MAIN, 1].rearrange("p (r i) -> p r i", r=R)))
            link(dve.tensor_tensor(used, used, bucket_base[:, :, 0:RT], ALU.subtract))

            with dve.Fori(ROOT1, R - 1) as r:
                buckets([(2 * r - 2 * ROOT1 + c, 2 * r - 2 * ROOT1 + c, t) for c in range(2) for t in range(T)],
                        r + 1, (1, 11))
            buckets([(R - 2, R - 2, t) for t in range(T)], R, (0, 5))
            add_spilled(0, R - 1)

            g = R - 1
            prepare(g, g, 0)
            low_of_unit(unit(ROOT2, 1))
            for t in range(T):
                if t + 1 < T:
                    prepare(g, g, t + 1)
                add(g, g, t)
                if t >= 2:
                    keep_root(STEPS * ROOT2 + t - 2, t - 2, 0, 2 + t % 2)
                for hh in range(2):
                    low_of_half(2 * T + 2 * t + hh, t, hh, relu=True)
            for t in (T - 2, T - 1):
                keep_root(STEPS * ROOT2 + t, t, 0, 2 + t % 2)
            for t in range(T):
                keep_root(STEPS * ROOT2 + T + t, t, 1, t % BANKS)
                if t == 3:
                    low_of_unit(unit(ROOT2 + 1, 0))

            dve.wait_ge(root_kept, 2 * STEPS)
            for t in range(T):
                dve.wait_ge(x_biased, t + 1)
                dve.tensor_tensor(acc[:, t, :], acc[:, t, :], x_rows[:, t % 2, :], ALU.add)\
                    .then_inc(residual_added, 1)
                if t == 1:
                    low_of_unit(unit(ROOT2 + 1, 1))
                if t == 6:
                    low_of_unit(unit(ROOT2 + 2, 0))
            dve.wait_ge(residual_added, T)
            with dve.Fori(1, R - 1) as r:
                buckets([(r + R - 1, r - 1, t) for t in range(T)], r + ROOT2 + 1, (0, 5))
            buckets([(2 * R - 2, R - 2, t) for t in range(T)], R + ROOT2, (0, 5), more=False)
            add_spilled(1, 2 * R - 1)

            def norm(t):
                dve.wait_ge(std_ready, t + 1)
                link(dve.reciprocal(std[:, t % 2, 1:2], std[:, t % 2, 0:1]))
                dve.tensor_scalar(acc[:, t, :], acc[:, t, :], moments[:, t % 2, 0:1], std[:, t % 2, 1:2],
                                  ALU.subtract, ALU.mult).then_inc(normed, 1)

            g = 2 * R - 1
            prepare(g, R - 1, 0, split=False)
            for t in range(T):
                if t + 1 < T:
                    prepare(g, R - 1, t + 1, split=False)
                add(g, R - 1, t)
                added(g, t)
                dve.bn_stats(stats[:, t % 2, 0, :], acc[:, t, 0:HALF])
                link(dve.bn_stats(stats[:, t % 2, 1, :], acc[:, t, HALF:D]))
                dve.bn_aggr(moments[:, t % 2, :], stats[:, t % 2].rearrange("p c s -> p (c s)"))\
                    .then_inc(var_ready, 1)
                if t:
                    norm(t - 1)
            norm(T - 1)


def kernel(x, src, dst, edge_type_8, L0_gnn_W1, L0_gnn_root1, L0_gnn_b1, L0_gnn_W2, L0_gnn_root2, L0_gnn_b2):
    import numpy as np
    import concourse.bacc as bacc
    from concourse.bass_utils import run_bass_kernel_spmd

    W1, W2 = np.asarray(L0_gnn_W1), np.asarray(L0_gnn_W2)
    half = W1.shape[0] // 2
    w_all = np.concatenate([W1[:half], np.asarray(L0_gnn_root1)[None], W1[half:],
                            np.asarray(L0_gnn_root2)[None], W2])
    arrays = {"x": x, "src": src, "dst": dst, "etype": edge_type_8, "w_all": w_all, "b1": L0_gnn_b1, "b2": L0_gnn_b2}
    arrays = {f"in_{k}": np.ascontiguousarray(v) for k, v in arrays.items()}
    nc = bacc.Bacc("TRN2", target_bir_lowering=False, num_devices=1)
    args = [nc.dram_tensor(k, v.shape, mybir.dt.from_np(v.dtype), kind="ExternalInput").ap()
            for k, v in arrays.items()]
    out = nc.dram_tensor("out", x.shape, mybir.dt.float32, kind="ExternalOutput").ap()
    rgcn_residual_layernorm(nc, *args, out)
    r = run_bass_kernel_spmd(nc, [arrays], core_ids=[0])
    return r.results[0]["out"]
```

```python
import math
from contextlib import ExitStack
from itertools import islice

import concourse.bass as bass
from concourse import mybir


def rgcn_residual_layernorm(nc, x, src, dst, etype, w_all, b1, b2, out):
    f32, f32r, bf16, i32 = mybir.dt.float32, mybir.dt.float32r, mybir.dt.bfloat16, mybir.dt.int32
    ALU, ACT, AX = mybir.AluOpType, mybir.ActivationFunctionType, mybir.AxisListType

    N, D = x.shape
    E = src.shape[0]
    Q = w_all.shape[0]
    R = Q // 2 - 1
    P = 128
    K = D // P
    HALF = D // 2
    T = -(-N // P)
    ROWS = [min(P, N - t * P) for t in range(T)]
    LOG_P = P.bit_length() - 1
    EP = max(p for p in range(1, P + 1) if E % p == 0)
    EJ = E // EP
    NB = R * T
    SEG = 2 * T

    def bucket_tiles(t):
        mean = ROWS[t] * E / N / R
        return math.ceil((mean + 3 * math.sqrt(mean)) / P)

    BT = bucket_tiles(0)
    BT_LAST = bucket_tiles(T - 1)
    assert all(bucket_tiles(t) == BT for t in range(T - 1)) and BT_LAST <= BT
    RT = BT * (T - 1) + BT_LAST
    MAIN = R * RT
    SPILL = -(-E // P)
    COLS = MAIN + SPILL
    FIRST = [BT * t for t in range(T)]
    END = FIRST[1:] + [RT]
    SLOT = [i % BT for i in range(RT)]
    NSPLIT = BT
    NRAW = 6
    RAW_USES = [len(range(s, RT, NRAW)) for s in range(NRAW)]
    IDX_CUT = (RT + 1) // 2
    STEPS = 2 * T
    BANKS = 4
    CJ = 10
    CHUNKS = EJ // CJ
    ROOT1 = R // 2
    MEAN1 = R
    ROOT2 = R + 1
    MEAN2 = Q - 1
    NEAR = 5
    EPS = 1e-5
    assert T % 2 == 0 and STEPS % BANKS == 0 and EJ % CJ == 0 and CHUNKS < STEPS and R == 8 and T == 10

    ctx = ExitStack()
    with ctx:
        def sb(name, shape, dt=f32):
            return ctx.enter_context(nc.sbuf_tensor(name, shape, dt))

        def sem(name):
            return ctx.enter_context(nc.semaphore(name))

        y = nc.dram_tensor("y", (R * N, D), f32).ap()
        table = nc.dram_tensor("edge_table", (P * COLS, 2), i32).ap()

        h_high = sb("h_high", [P, K, T * P], f32r)
        h_low = sb("h_low", [P, K, T * P], f32r)
        w_high = sb("w_high", [P, 2, K, HALF], f32r)
        w_low = sb("w_low", [P, 2, K, HALF], f32r)
        w_raw = sb("w_raw", [P, K, HALF])
        y_stage = sb("y_stage", [P, BANKS, HALF])
        one_hot = sb("one_hot", [P, 2, BT, P], f32r)
        bias = sb("bias", [P, 2, D])
        edges = sb("edges", [P, COLS, 2], i32)
        dst_local = sb("dst_local", [P, R, BT * T])
        bucket_gid = sb("bucket_gid", [P, R, BT * T], i32)
        bucket_base = sb("bucket_base", [P, R, BT * T])
        inv_count = sb("inv_count", [P, NB])
        index_a = sb("index_a", [P, IDX_CUT], i32)
        index_b = sb("index_b", [P, RT - IDX_CUT], i32)
        identity = sb("identity", [P, P])
        column = sb("column", [P, P], bf16)
        column_i = sb("column_i", [P, P], i32)
        before = sb("before", [P, P], bf16)
        ones = sb("ones", [P, P], bf16)
        eps = sb("eps", [P, 1])
        stats = sb("stats", [P, 2, 2, 6])
        moments = sb("moments", [P, 2, 2])
        std = sb("std", [P, 2, 2])
        spill_n = sb("spill_n", [P, 1], i32)
        spill_index = sb("spill_index", [P, 1], i32)
        spill_gid = sb("spill_gid", [P, 1])
        payload = sb("payload", [EP, EJ, 2], i32)
        position = sb("position", [EP, EJ], i32)
        dl_bf = sb("dl_bf", [EP, EJ], bf16)
        key_bf = sb("key_bf", [EP, EJ], bf16)
        small = sb("small", [P, 4, NB])
        small_bf = sb("small_bf", [P, 3, NB], bf16)
        edge_i = sb("edge_i", [EP, 4, EJ], i32)
        top = nc.sbuf_base if isinstance(nc.sbuf_base, int) else nc.sbuf_base()
        region = sb("region", [P, (T + NRAW + 2 * NSPLIT + 2) * D])
        base = -(-top // 32) * 32

        def at(name, shape, dt, offset):
            return nc.alloc_sbuf_tensor_at(name, shape, dt, offset=base + offset * 4)

        A0, G0, X0 = 0, T * D, (T + NRAW + 2 * NSPLIT) * D
        acc = at("acc", [P, T, D], f32, A0)
        raw = at("raw", [P, NRAW, D], f32, G0)
        g_high = at("g_high", [P, NSPLIT, D], f32r, G0 + NRAW * D)
        g_low = at("g_low", [P, NSPLIT, D], f32r, G0 + (NRAW + NSPLIT) * D)
        x_rows = at("x_rows", [P, 2, D], f32, X0)
        is_key = at("is_key", [EP, NB, EJ], bf16, G0)
        assert NB * EJ * 2 <= (NRAW + 2 * NSPLIT) * D * 4
        ranks = at("ranks", [EP, SEG, EJ], f32, A0)
        go_on = at("go_on", [EP, SEG, EJ], bf16, A0 + SEG * EJ)
        EF = A0 + -(-SEG * EJ * 3 // 16) * 8
        edge_f = at("edge_f", [EP, 12, EJ], f32, EF)
        assert EF + 12 * EJ <= T * D
        dst_hot = at("dst_hot", [EP, 2, CJ, P], bf16, X0)
        assert 2 * CJ * P * 2 <= 2 * D * 4

        prod = ctx.enter_context(nc.psum_tensor("prod", [P, BANKS, 512], f32))
        agg = ctx.enter_context(nc.psum_tensor("agg", [P, 2, 2, 512], f32))

        def turned(n, hh, t):
            return agg[:, t % 2, hh, 0:HALF] if n == 0 else prod[:, hh, 0:HALF]

        consts_set = sem("consts_set")
        keys_loaded = sem("keys_loaded")
        x_copied = sem("x_copied")
        relu_done = sem("relu_done")
        h_stored = sem("h_stored")
        x_loaded = [sem(f"x_loaded{s}") for s in range(2)]
        bias_loaded = sem("bias_loaded")
        table_cleared = sem("table_cleared")
        dve_step = sem("dve_step")
        pool_step = sem("pool_step")
        rows_counted = sem("rows_counted")
        rows_summed = sem("rows_summed")
        flags_counted = sem("flags_counted")
        flags_summed = sem("flags_summed")
        positions_ready = sem("positions_ready")
        scattered = sem("scattered")
        table_loaded = sem("table_loaded")
        index_loaded = sem("index_loaded")
        hot_ready = sem("hot_ready")
        chunk_counted = sem("chunk_counted")
        transposed = sem("transposed")
        h_high_ready = sem("h_high_ready")
        h_low_ready = sem("h_low_ready")
        w_loaded = sem("w_loaded")
        w_high_ready = sem("w_high_ready")
        w_low_ready = sem("w_low_ready")
        prod_done = sem("prod_done")
        y_staged = sem("y_staged")
        y_stored = [sem(f"y_stored{s}") for s in range(BANKS)]
        root_kept = sem("root_kept")
        raw_loaded = [sem(f"raw_loaded{s}") for s in range(NRAW)]
        high_ready = sem("high_ready")
        low_ready = sem("low_ready")
        one_hot_ready = sem("one_hot_ready")
        tile_used = sem("tile_used")
        bucket_added = sem("bucket_added")
        residual_loaded = [sem(f"residual_loaded{s}") for s in range(2)]
        x_biased = sem("x_biased")
        residual_added = sem("residual_added")
        var_ready = sem("var_ready")
        std_ready = sem("std_ready")
        normed = sem("normed")
        out_stored = sem("out_stored")
        spill_copied = [sem(f"spill_copied{l}") for l in range(2)]
        spill_shifted = [sem(f"spill_shifted{l}") for l in range(2)]
        spill_loaded = [sem(f"spill_loaded{l}") for l in range(2)]
        spill_high = [sem(f"spill_high{l}") for l in range(2)]
        spill_low = [sem(f"spill_low{l}") for l in range(2)]
        spill_hot = [sem(f"spill_hot{l}") for l in range(2)]
        spill_summed = [sem(f"spill_summed{l}") for l in range(2)]
        spill_added = [sem(f"spill_added{l}") for l in range(2)]

        spill_averaged = [sem(f"spill_averaged{l}") for l in range(2)]
        spill_turned = [sem(f"spill_turned{l}") for l in range(2)]
        spill_turned_high = [sem(f"spill_turned_high{l}") for l in range(2)]
        spill_turned_low = [sem(f"spill_turned_low{l}") for l in range(2)]
        spill_multiplied = [sem(f"spill_multiplied{l}") for l in range(2)]

        def unit(q, h):
            return 2 * q + h

        def stored_before(layer, r):
            return layer * (R - 1) + r - 1

        def two_relations(g, r):
            return lambda s: [("sum", g + s // T, r + s // T, s % T)]

        def one_relation(g, r):
            return lambda s: [("sum", g, r, t) for t in range(T) if s == 3 + (STEPS - 4) * t // (T - 1)]

        def averaging(g, r, n):
            def actions(s):
                todo = [("sum", g, r, t) for t in range(T) if s == 2 + (4 * t + 3) // 5]
                if s >= T:
                    todo.append(("average", g + 1, 0, s - T))
                if s > T:
                    todo.append(("turn", n, None, s - T - 1))
                return todo
            return actions

        def completing(s):
            turn = [("turn", 1, None, T - 1)] if s == 0 else [("turn", 2, None, s - T - 1)] if s > T else []
            return [("sum", R - 2 + s // T, R - 2 + s // T, s % T)] + turn

        def turning_x(s):
            return [("turn", 0, None, s + 2)] if s + 2 < T else []

        def last_turn(s):
            return [("turn", 2, None, T - 1)] if s == 0 else []

        def finishing(s):
            if s == 0:
                return [("turn", 3, None, T - 1)]
            return [("sum", 2 * R - 1, R - 1, s - 3)] if 3 <= s < T + 3 else []

        SPILL_STEP = (T - 1, 2)

        def banks(shift, turning=False):
            return lambda s: 2 + s % 2 if turning and s >= T else (s + shift) % BANKS

        block = ctx.enter_context(nc.Block())

        @block.sync
        def _(sp):
            def load_unit(q, h):
                u = unit(q, h)
                if not (isinstance(q, int) and u == 0):
                    sp.wait_ge(w_high_ready, u)
                    sp.wait_ge(w_low_ready, u)
                w = w_all[bass.ds(q, 1), :, h * HALF:(h + 1) * HALF].rearrange("o (k p) n -> p (o k) n", p=P)
                sp.dma_start(w_raw[:], w).then_inc(w_loaded, 16)

            def store_y(yc, r, s):
                h, t = divmod(s, T)
                sp.wait_ge(y_staged, STEPS * yc + s + 1)
                sp.dma_start(y[bass.ds(r * N + t * P, ROWS[t]), h * HALF:(h + 1) * HALF],
                             y_stage[0:ROWS[t], s % BANKS, :]).then_inc(y_stored[s % BANKS], 16)

            def relation(q, yc, r):
                for s in range(STEPS):
                    store_y(yc, r, s)
                    if s == 8:
                        load_unit(q + 1, 0)
                    if s == 14:
                        load_unit(q + 1, 1)

            def load_x(t):
                if t >= 2:
                    sp.wait_ge(transposed, 2 * (t - 1))
                sp.dma_start(x_rows[0:ROWS[t], t % 2, :],
                             x[t * P:t * P + ROWS[t], :]).then_inc(x_loaded[t % 2], 16)

            load_unit(0, 0)
            load_x(0)
            load_x(1)
            for n, a in enumerate((dst, etype, src)):
                sp.dma_start(edge_i[:, n, :], a.rearrange("(p j) -> p j", p=EP)).then_inc(keys_loaded, 16)
            load_x(2)
            load_x(3)
            load_unit(0, 1)
            for n, b in enumerate((b1, b2)):
                sp.dma_start(bias[:, n, :], b.rearrange("(o n) -> o n", o=1).to_broadcast([P, D]))\
                    .then_inc(bias_loaded, 16)
            sp.wait_ge(consts_set, 1)
            sp.dma_start(table.rearrange("(p c) w -> p (c w)", p=P),
                         edges[:].rearrange("p c w -> p (c w)")).then_inc(table_cleared, 16)


            for s in range(STEPS):
                store_y(0, 1, s)
                if s + 4 < T:
                    load_x(s + 4)
                if s == 8:
                    load_unit(1, 0)
                if s == 14:
                    load_unit(1, 1)
                if s == STEPS - 1:
                    sp.dma_start(y[0:N, :], x).then_inc(x_copied, 16)
            with sp.Fori(1, ROOT1) as q:
                relation(q, q, q + 1)
            load_unit(ROOT1 + 1, 0)
            sp.wait_ge(scattered, 16 * EJ)
            sp.dma_start(edges[:].rearrange("p c w -> p (c w)"),
                         table.rearrange("(p c) w -> p (c w)", p=P)).then_inc(table_loaded, 16)
            load_unit(ROOT1 + 1, 1)
            with sp.Fori(ROOT1 + 1, R) as q:
                relation(q, q - 1, q)
            load_unit(ROOT2, 0)
            load_unit(ROOT2, 1)
            for t in range(T):
                sp.wait_ge(relu_done, t + 1)
                sp.dma_start(y[t * P:t * P + ROWS[t], :], acc[0:ROWS[t], t, :]).then_inc(h_stored, 16)
            load_unit(ROOT2 + 1, 0)
            load_unit(ROOT2 + 1, 1)

            sp.wait_ge(transposed, 4 * T)
            for t in range(T):
                if t >= 2:
                    sp.wait_ge(residual_added, t - 1)
                sp.dma_start(x_rows[0:ROWS[t], t % 2, :],
                             x[t * P:t * P + ROWS[t], :]).then_inc(residual_loaded[t % 2], 16)
                for s in (2 * t, 2 * t + 1):
                    store_y(R - 1, 1, s)
                    if s == 4:
                        load_unit(ROOT2 + 2, 0)
                    if s == 14:
                        load_unit(ROOT2 + 2, 1)
            with sp.Fori(2, R) as r:
                relation(r + ROOT2, stored_before(1, r), r)
            for t in range(T):
                sp.wait_ge(normed, t + 1)
                sp.dma_start(out[t * P:t * P + ROWS[t], :], acc[0:ROWS[t], t, :]).then_inc(out_stored, 16)
            sp.wait_ge(out_stored, 16 * T)

        @block.gpsimd
        def _(pool):
            steps = [0]

            def link(ins):
                steps[0] += 1
                ins.then_inc(pool_step, 1)
                pool.wait_ge(pool_step, steps[0])

            pool.memset(edges[:, :, 0], R * N)
            link(pool.memset(edges[:, :, 1], -1))
            pool.memset(before[:], 1.0)
            pool.memset(ones[:], 1.0)
            pool.memset(eps[:], EPS)
            pool.iota(column_i[:], [[1, P]], base=0, channel_multiplier=0)
            pool.iota(bucket_gid[:].rearrange("p r (t b) -> p r t b", b=BT),
                      [[T * P, R], [P, T], [0, BT]], base=0, channel_multiplier=0)
            link(pool.memset(identity[:], 0.0))
            pool.affine_select(out=identity[:], in_=identity[:], compare_op=ALU.not_equal, fill=1.0, base=0,
                               pattern=[[-1, P]], channel_multiplier=1)
            link(pool.affine_select(out=before[:], in_=before[:], compare_op=ALU.is_gt, fill=0.0, base=0,
                                    pattern=[[1, P]], channel_multiplier=-1))
            pool.nop().then_inc(consts_set, 1)
            row_limit = pool.to_reg(R * N - 1)

            def low_of_unit(q, h):
                u = unit(q, h)
                pool.wait_ge(w_high_ready, u + 1)
                pool.tensor_tensor(w_low[:, h], w_raw[:], w_high[:, h].bitcast(f32), ALU.subtract)\
                    .then_inc(w_low_ready, 1)

            def wait_both(semaphore, value):
                value = value if isinstance(value, int) else pool.snap(pool.to_reg(value))
                pool.wait_ge(table_loaded, 16)
                pool.wait_ge(semaphore, value)

            def load_index(part, r, count):
                buf, first = ((index_a, 0), (index_b, IDX_CUT))[part]
                n = buf.shape[1]
                pool.tensor_copy(buf[:], edges[:, bass.ds(r * RT + first, n), 0]).then_inc(index_loaded, 1)
                wait_both(index_loaded, count)

            def wait_y(layer, r):
                for s in range(BANKS):
                    pool.wait_ge(y_stored[s], 16 * (STEPS // BANKS) * (stored_before(layer, r) + 1))

            def gather(g, r, i, written, following):
                slot = i % NRAW
                prev = i - NRAW if i >= NRAW else max(range(slot, RT, NRAW)) - RT
                wait_both(low_ready, NRAW + RT * g + prev + 1)
                if i == NRAW + 1:
                    load_index(1, r, 2 * g + 2)
                if i == IDX_CUT + NRAW + 1 and following is not None:
                    load_index(0, following, 2 * g + 3)
                col = index_a[:, i:i + 1] if i < IDX_CUT else index_b[:, i - IDX_CUT:i - IDX_CUT + 1]
                pool.indirect_dma_start(raw[:, slot, :], None, y[0:written * N, :],
                                        bass.IndirectOffsetOnAxis(ap=col, axis=0),
                                        bounds_check=row_limit, oob_is_err=False)\
                    .then_inc(raw_loaded[slot], 16)

            def gather_relation(g, r, following, written=R):
                for i in range(RT):
                    gather(g, r, i, written, following)

            def gather_spilled(layer, g):
                n = pool.value_load(spill_n[0:1, 0:1], min_val=0, max_val=SPILL)
                with pool.If(n > 0):
                    pool.wait_ge(low_ready, NRAW + RT * g)
                    wait_y(layer, R - 1)
                    with pool.Fori(0, n) as i:
                        pool.wait_ge(spill_added[layer], NB * i + 1)
                        pool.tensor_copy(spill_index[:], edges[:, bass.ds(i + MAIN, 1), 0])\
                            .then_inc(spill_copied[layer], 1)
                        wait_both(spill_copied[layer], i + 1)
                        pool.indirect_dma_start(raw[:, 0, :], None, y,
                                                bass.IndirectOffsetOnAxis(ap=spill_index[:], axis=0),
                                                bounds_check=row_limit, oob_is_err=False)\
                            .then_inc(spill_loaded[layer], 16)
                    pool.wait_ge(spill_added[layer], NB * n + 1)
                pool.end_ifs()

            for u in range(1, NEAR):
                low_of_unit(u // 2, u % 2)
            pool.wait_ge(table_cleared, 16)
            pool.wait_ge(positions_ready, 1)
            for j in range(EJ):
                pool.indirect_dma_start(table, bass.IndirectOffsetOnAxis(ap=position[:, j:j + 1], axis=0),
                                        payload[:, j, :], None).then_inc(scattered, 16)
            pool.wait_ge(scattered, 16 * EJ)
            pool.wait_ge(chunk_counted, CHUNKS)
            link(pool.memset(raw[:], 0.0))
            pool.wait_ge(table_loaded, 16)
            load_index(0, 1, 1)

            pool.wait_ge(x_copied, 16)
            wait_y(0, ROOT1)
            with pool.Fori(0, ROOT1) as g:
                gather_relation(g, g + 1, g + 2, ROOT1 + 1)
            wait_y(0, ROOT1 + 1)
            gather_relation(R - 4, R - 3, 0, R - 2)
            gather_relation(R - 3, 0, R - 2, R - 2)
            wait_y(0, R - 2)
            gather_relation(R - 2, R - 2, R - 1, R - 1)
            gather_spilled(0, R - 1)
            wait_y(0, R - 1)
            gather_relation(R - 1, R - 1, 1)

            for t in range(T):
                pool.wait_ge(residual_loaded[t % 2], 16 * (t // 2 + 1))
                pool.wait_ge(bias_loaded, 32)
                pool.tensor_tensor(x_rows[:, t % 2, :], x_rows[:, t % 2, :], bias[:, 1, :], ALU.add)\
                    .then_inc(x_biased, 1)
            with pool.Fori(1, R - 2) as r:
                wait_y(1, r)
                gather_relation(r + R - 1, r, r + 1)
            wait_y(1, R - 2)
            gather_relation(2 * R - 3, R - 2, 0)
            pool.wait_ge(h_stored, 16 * T)
            gather_relation(2 * R - 2, 0, R - 1)
            gather_spilled(1, 2 * R - 1)
            wait_y(1, R - 1)
            gather_relation(2 * R - 1, R - 1, None)

        @block.scalar
        def _(act):
            def high_of_unit(q, h):
                u = unit(q, h)
                act.wait_ge(w_loaded, 16 * (u + 1))
                if not (isinstance(q, int) and q == 0):
                    act.wait_ge(prod_done, T * (u - 1))
                act.activation(w_high[:, h], w_raw[:], ACT.Copy).then_inc(w_high_ready, 1)

            def high_of_tile(g, i):
                slot = i % NRAW
                act.wait_ge(raw_loaded[slot], 16 * (RAW_USES[slot] * g + i // NRAW + 1))
                prev = i - NSPLIT if i >= NSPLIT else max(range(SLOT[i], RT, NSPLIT)) - RT
                act.wait_ge(tile_used, NSPLIT + RT * g + prev + 1)
                act.activation(g_high[:, SLOT[i], :], raw[:, slot, :], ACT.Copy).then_inc(high_ready, 1)

            def bucket(g, t):
                for i in range(FIRST[t], END[t]):
                    high_of_tile(g, i)

            def high_of_turn(n, t):
                for hh in range(2):
                    u = 2 * T * n + 2 * t + hh
                    act.wait_ge(transposed, u + 1)
                    act.activation(h_high[:, 3 * hh:3 * hh + 3, t * P:(t + 1) * P],
                                   turned(n, hh, t).rearrange("p (k n) -> p k n", n=P), ACT.Copy)\
                        .then_inc(h_high_ready, 1)

            def relu(t):
                act.wait_ge(bucket_added, 2 + T * (R - 1) + t + 1)
                act.wait_ge(root_kept, STEPS + T + t + 1)
                act.activation(acc[:, t, :], acc[:, t, :], ACT.Relu).then_inc(relu_done, 1)

            def stage_y(yc, k, s, bank):
                act.wait_ge(prod_done, k + 1)
                if not (isinstance(yc, int) and yc == 0 and s < BANKS):
                    act.wait_ge(y_stored[s % BANKS], 16 * ((STEPS // BANKS) * yc + s // BANKS))
                act.activation(y_stage[:, s % BANKS, :], prod[:, bank, 0:HALF], ACT.Copy)\
                    .then_inc(y_staged, 1)

            def matrix(q, yc, bank, actions=lambda s: [], more=True, spilled=None, ahead=False, high_at=1):
                cut = SPILL_STEP[spilled[0]] if spilled else -1
                order = [(s, a) for s in range(STEPS) for a in actions(s) if a[0] != "turn"]
                ready = n = 0
                for s in range(STEPS):
                    sums = sum(a[0] != "turn" for a in actions(s))
                    turns = [a for a in actions(s) if a[0] == "turn"]
                    n += sums
                    if not ahead or ready == 0:
                        for m in range(ready, n):
                            bucket(order[m][1][1], order[m][1][3])
                        ready = n
                    if yc is not None:
                        stage_y(yc, STEPS * q + s, s, bank(s))
                    for _, turn, _, t in turns:
                        if turn == 2:
                            relu(t)
                    if ahead and sums:
                        last = min(n + 1, len(order))
                        last -= last > n and s <= cut < order[n][0]
                        for m in range(ready, last):
                            bucket(order[m][1][1], order[m][1][3])
                        ready = last
                    for _, turn, _, t in turns:
                        high_of_turn(turn, t)
                    if s == high_at:
                        high_of_unit(q, 1)
                    if s == 11 and more:
                        high_of_unit(q + 1, 0)
                    if s == cut:
                        high_spilled(*spilled)

            def high_spilled(layer, g):
                act.wait_ge(positions_ready, 1)
                n = act.value_load(spill_n[0:1, 0:1], min_val=0, max_val=SPILL)
                with act.If(n > 0):
                    act.wait_ge(tile_used, NSPLIT + RT * g)
                    with act.Fori(0, n) as i:
                        act.wait_ge(spill_loaded[layer], i * 16 + 16)
                        act.activation(g_high[:, 0, :], raw[:, 0, :], ACT.Copy).then_inc(spill_high[layer], 1)
                        for t in range(T):
                            act.wait_ge(spill_turned[layer], i * T + t + 1)
                            act.activation(g_high[:, 1, :].rearrange("p (c n) -> p c n", c=2),
                                           prod[:, 0:2, 0:HALF], ACT.Copy).then_inc(spill_turned_high[layer], 1)
                act.end_ifs()

            high_of_unit(0, 0)
            high_of_turn(0, 0)
            high_of_turn(0, 1)
            matrix(0, 0, banks(0), turning_x)
            with act.Fori(1, ROOT1) as q:
                matrix(q, q, banks(0))
            high_of_unit(ROOT1, 1)
            high_of_unit(ROOT1 + 1, 0)
            with act.Fori(ROOT1 + 1, R - 1) as q:
                matrix(q, q - 1, banks(0), two_relations(2 * q - 2 * ROOT1 - 2, 0))
            matrix(R - 1, R - 2, banks(0, True), averaging(R - 4, None, 1), ahead=True, high_at=4)
            matrix(MEAN1, None, None, completing, spilled=(0, R - 1), ahead=True)
            matrix(ROOT2, None, None, last_turn)
            matrix(ROOT2 + 1, R - 1, banks(2))
            with act.Fori(2, R - 1) as r:
                matrix(r + ROOT2, stored_before(1, r), banks(2), one_relation(r + R - 2, None))
            matrix(MEAN2 - 1, 2 * R - 3, banks(2, True), averaging(2 * R - 3, None, 3), ahead=True, high_at=4)
            matrix(MEAN2, None, None, finishing, more=False, spilled=(1, 2 * R - 1), high_at=0)
            for t in range(T):
                act.wait_ge(var_ready, t + 1)
                act.activation(std[:, t % 2, 0:1], moments[:, t % 2, 1:2], ACT.Sqrt, bias=eps[:])\
                    .then_inc(std_ready, 1)

        @block.tensor
        def _(pe):
            def transpose_half(rows, hh, bank):
                for k in range(3):
                    c = 3 * hh + k
                    mm = pe.transpose(bank[:, k * P:(k + 1) * P], rows[:, c * P:(c + 1) * P], identity[:])
                mm.then_inc(transposed, 1)

            def product(q, h, t, bank):
                n = K * 3
                for k in range(K):
                    for left, right in ((h_high, w_high), (h_high, w_low), (h_low, w_high)):
                        n -= 1
                        mm = pe.matmul(prod[:, bank, 0:HALF], left[:, k, t * P:(t + 1) * P], right[:, h, k, :],
                                       start=(k == 0 and left is h_high and right is w_high), stop=(n == 0))
                return mm

            def unit_ready(q, h):
                pe.wait_ge(w_high_ready, unit(q, h) + 1)
                pe.wait_ge(w_low_ready, unit(q, h) + 1)

            def step(q, s, bank, free):
                h, t = divmod(s, T)
                if t == 0:
                    unit_ready(q, h)
                for wait in free:
                    pe.wait_ge(*wait)
                product(q, h, t, bank).then_inc(prod_done, 1)

            def bucket(g, t):
                par = t % 2
                pe.wait_ge(bucket_added, T * g + t + 1)
                pe.wait_ge(one_hot_ready, T * g + t + 1)
                last = END[t] - 1
                for i in range(FIRST[t], END[t]):
                    pe.wait_ge(low_ready, NRAW + RT * g + i + 1)
                    for part in (g_high, g_low):
                        for c in range(2):
                            mm = pe.matmul(agg[:, par, c, 0:HALF], one_hot[:, par, i - FIRST[t], :],
                                           part[:, SLOT[i], c * HALF:(c + 1) * HALF],
                                           start=(i == FIRST[t] and part is g_high),
                                           stop=(i == last and part is g_low), skip_group_check=True)
                    mm.then_inc(tile_used, 1)

            def sum_rows():
                pe.wait_ge(rows_counted, 1)
                pe.matmul(agg[:, 1, 0, 0:NB], before[0:EP, :], small_bf[0:EP, 1, :], start=True, stop=True)\
                    .then_inc(rows_summed, 1)

            def sum_flags():
                pe.wait_ge(flags_counted, 1)
                pe.matmul(agg[:, 1, 0, 0:1], before[0:EP, :], small_bf[0:EP, 2, 0:1], start=True, stop=True)
                pe.matmul(agg[:, 1, 1, 0:1], ones[0:EP, :], small_bf[0:EP, 2, 0:1], start=True, stop=True)\
                    .then_inc(flags_summed, 1)

            def sum_spilled(layer, g):
                kept_steps = STEPS * (1 + 2 * layer) + SPILL_STEP[layer] + 1
                q = (MEAN1, MEAN2)[layer]
                pe.wait_ge(positions_ready, 1)
                n = pe.value_load(spill_n[0:1, 0:1], min_val=0, max_val=SPILL)

                def sum_bucket(i, key):
                    pe.wait_ge(spill_low[layer], i + 1)
                    pe.wait_ge(spill_hot[layer], i * NB + key + 1)
                    for part in (g_high, g_low):
                        for c in range(2):
                            mm = pe.matmul(agg[:, 0, c, 0:HALF], one_hot[:, 0, 0, :],
                                           part[:, 0, c * HALF:(c + 1) * HALF],
                                           start=part is g_high, stop=part is g_low, skip_group_check=True)
                    mm.then_inc(spill_summed[layer], 1)

                with pe.If(n > 0):
                    pe.wait_ge(bucket_added, 2 + T * g)
                    pe.wait_ge(root_kept, kept_steps)
                    pe.wait_ge(h_low_ready, 2 * T * (2 + 2 * layer))
                    unit_ready(q, 1)
                    with pe.Fori(0, n) as i:
                        for t in range(T):
                            sum_bucket(i, t)
                            pe.wait_ge(spill_averaged[layer], i * T + t + 1)
                            for c in range(K):
                                mm = pe.transpose(prod[:, c // 3, c % 3 * P:(c % 3 + 1) * P],
                                                  x_rows[:, 0, c * P:(c + 1) * P], identity[:])
                            mm.then_inc(spill_turned[layer], 1)
                            pe.wait_ge(spill_turned_low[layer], i * T + t + 1)
                            for h in range(2):
                                for k in range(K):
                                    cut = slice(k * P, (k + 1) * P)
                                    for left, right in ((g_high, w_high), (g_high, w_low), (g_low, w_high)):
                                        mm = pe.matmul(prod[:, 2 + h, 0:HALF], left[:, 1, cut], right[:, h, k, :],
                                                       start=(k == 0 and left is g_high and right is w_high),
                                                       stop=(k == K - 1 and left is g_low))
                            mm.then_inc(spill_multiplied[layer], 1)
                        with pe.Fori(1, R) as r:
                            for t in range(T):
                                sum_bucket(i, r * T + t)
                pe.end_ifs()

            def turn(n, t):
                if n == 0:
                    pe.wait_ge(x_loaded[t % 2], 16 * (t // 2 + 1))
                elif n == 2:
                    pe.wait_ge(relu_done, t + 1)
                else:
                    g = R - 3 if n == 1 else 2 * R - 2
                    pe.wait_ge(bucket_added, 2 + T * g + t + 1)
                rows = acc[:, t, :] if n == 2 else x_rows[:, t % 2, :]
                for hh in range(2):
                    u = 2 * T * n + 2 * t + hh
                    if t >= (1 if n else 2):
                        pe.wait_ge(h_low_ready, u - (1 if n else 3))
                    elif n == 2:
                        pe.wait_ge(root_kept, STEPS + T)
                    elif n:
                        pe.wait_ge(y_staged, STEPS * (R - 2 if n == 1 else 2 * R - 3) + T)
                    transpose_half(rows, hh, turned(n, hh, t))

            def staged(yc, turning=False):
                def free(s):
                    if isinstance(yc, int) and yc == 0 and s < BANKS:
                        return []
                    return [(y_staged, STEPS * yc + s + 1 - (2 if turning and s >= T else BANKS))]
                return free

            def kept(base, before, n=None, turning=False):
                def free(s):
                    wait = [(h_low_ready, 2 * T * n + 2 * s + 2)] if n is not None and s < T else []
                    if s < 2 and n is not None:
                        return wait + [(before[0], before[1] - 1 + s)]
                    if s < BANKS:
                        return wait + [(h_low_ready, 2 * T * (n + 1))]
                    return wait + [(root_kept, base + s + 1 - (2 if turning and s >= T else BANKS))]
                return free

            def matrix(q, bank, free, actions=lambda s: [], spilled=None, middle=None):
                for s in range(STEPS):
                    if s == STEPS - 2 and middle:
                        middle()
                    step(q, s, bank(s), free(s))
                    for what, a, _, t in actions(s):
                        if what == "turn":
                            turn(a, t)
                        else:
                            bucket(a, t)
                    if spilled and s == SPILL_STEP[spilled[0]]:
                        sum_spilled(*spilled)

            pe.wait_ge(pool_step, 3)
            pe.wait_ge(consts_set, 1)
            pe.nop().then_inc(tile_used, NSPLIT)
            turn(0, 0)
            turn(0, 1)
            matrix(0, banks(0), lambda s: staged(0)(s) + ([(h_low_ready, 2 * s + 2)] if s < T else []), turning_x,
                   middle=sum_rows)
            matrix(1, banks(0), staged(1), middle=sum_flags)
            with pe.Fori(2, ROOT1) as q:
                matrix(q, banks(0), staged(q))
            for s in range(STEPS):
                step(ROOT1, s, s % BANKS, [(y_staged, STEPS * ROOT1 - BANKS + s + 1) if s < BANKS
                                           else (root_kept, s - BANKS + 1)])
                if s < CHUNKS:
                    pe.wait_ge(hot_ready, s + 1)
                    for j in range(CJ):
                        e = s * CJ + j
                        mm = pe.matmul(agg[:, 0, 0, 0:NB], dst_hot[:, s % 2, j, :], is_key[:, :, e],
                                       start=(e == 0), stop=(e == EJ - 1))
                    mm.then_inc(chunk_counted, 1)
            pe.wait_ge(root_kept, STEPS)
            with pe.Fori(ROOT1 + 1, R - 1) as q:
                matrix(q, banks(0), staged(q - 1), two_relations(2 * q - 2 * ROOT1 - 2, 0))
            matrix(R - 1, banks(0, True), staged(R - 2, True), averaging(R - 4, None, 1))
            matrix(MEAN1, banks(2, True), kept(STEPS, (y_staged, STEPS * (R - 1)), 1, True), completing,
                   spilled=(0, R - 1))

            matrix(ROOT2, banks(2), kept(2 * STEPS, (root_kept, 2 * STEPS), 2), last_turn)
            matrix(ROOT2 + 1, banks(2), lambda s: [(root_kept, 3 * STEPS - BANKS + s + 1)] if s < BANKS
                   else staged(R - 1)(s))
            with pe.Fori(2, R - 1) as r:
                matrix(r + ROOT2, banks(2), staged(stored_before(1, r)), one_relation(r + R - 2, None))
            matrix(MEAN2 - 1, banks(2, True), staged(2 * R - 3, True), averaging(2 * R - 3, None, 3))
            matrix(MEAN2, banks(2), kept(3 * STEPS, (y_staged, 2 * STEPS * (R - 1)), 3), finishing,
                   spilled=(1, 2 * R - 1))

        @block.vector
        def _(dve):
            steps = [0]

            def link(ins):
                steps[0] += 1
                ins.then_inc(dve_step, 1)
                dve.wait_ge(dve_step, steps[0])

            def low_of_unit(u, h=None):
                dve.wait_ge(w_high_ready, u + 1)
                if isinstance(u, int) and u == NEAR:
                    dve.wait_ge(w_low_ready, u)
                h = h if h is not None else u % 2
                dve.tensor_tensor(w_low[:, h], w_raw[:], w_high[:, h].bitcast(f32), ALU.subtract)\
                    .then_inc(w_low_ready, 1)

            def low_of_half(u, t, psum):
                k = 3 * (u % 2)
                psum = psum.rearrange("p (k n) -> p k n", n=P)
                high = h_high[:, k:k + 3, t * P:(t + 1) * P].bitcast(f32)
                low = h_low[:, k:k + 3, t * P:(t + 1) * P]
                dve.wait_ge(h_high_ready, u + 1)
                dve.tensor_tensor(low, psum, high, ALU.subtract).then_inc(h_low_ready, 1)

            def keep(k, t, h, bank, plus):
                dve.wait_ge(prod_done, k + 1)
                a = acc[:, t, h * HALF:(h + 1) * HALF]
                if plus is None:
                    ins = dve.tensor_copy(a, prod[:, bank, 0:HALF])
                else:
                    b = a if plus == "acc" else bias[:, 0, h * HALF:(h + 1) * HALF]
                    ins = dve.tensor_tensor(a, prod[:, bank, 0:HALF], b, ALU.add)
                ins.then_inc(root_kept, 1)

            def prepare(g, r, t):
                par = t % 2
                dve.wait_ge(tile_used, NSPLIT + RT * g + (END[t - 2] if t >= 2 else END[T - 2 + t] - RT))
                for i in range(FIRST[t], END[t]):
                    ins = dve.tensor_scalar(one_hot[:, par, i - FIRST[t], :], column[:],
                                            dst_flat[:, bass.ds(r * BT * T + i, 1)], None, ALU.is_equal)
                ins.then_inc(one_hot_ready, 1)
                for i in range(FIRST[t], END[t]):
                    dve.wait_ge(high_ready, RT * g + i + 1)
                    dve.tensor_tensor(g_low[:, SLOT[i], :], raw[:, i % NRAW, :],
                                      g_high[:, SLOT[i], :].bitcast(f32), ALU.subtract).then_inc(low_ready, 1)

            def add(g, r, t):
                dve.wait_ge(tile_used, NSPLIT + RT * g + END[t])
                a = acc[:, t, :].rearrange("p (c n) -> p c n", c=2)
                dve.scalar_tensor_tensor(a, agg[:, t % 2, :, 0:HALF], inv_count[:, bass.ds(r * T + t, 1)], a,
                                         ALU.mult, ALU.add).then_inc(bucket_added, 1)

            def average(g, t):
                n = 1 if g < R else 3
                dve.wait_ge(tile_used, NSPLIT + RT * g + END[t])
                if t >= 2:
                    dve.wait_ge(transposed, 2 * T * n + 2 * (t - 1))
                dve.tensor_scalar(x_rows[:, t % 2, :].rearrange("p (c n) -> p c n", c=2),
                                  agg[:, t % 2, :, 0:HALF], inv_count[:, t:t + 1], None, ALU.mult)\
                    .then_inc(bucket_added, 1)

            def added(g, t):
                dve.wait_ge(bucket_added, 2 + T * g + t + 1)

            def low_of_turn(n, t):
                for hh in range(2):
                    u = 2 * T * n + 2 * t + hh
                    low_of_half(u, t, turned(n, hh, t))

            def matrix(q, actions, keep_step=None, more=True, spilled=None, after=None, low_at=2):
                cut = SPILL_STEP[spilled[0]] if spilled else -1
                order = [(s, a[1:]) for s in range(STEPS) for a in actions(s) if a[0] != "turn"]
                ready = n = 0

                def prepare_next():
                    prepare(*order[n][1])
                    return n + 1

                for s in range(STEPS):
                    if keep_step and order[0][0] == s == 0:
                        ready = prepare_next()
                    if keep_step:
                        keep_step(s)
                    for what, *a in actions(s):
                        if what == "turn":
                            low_of_turn(a[0], a[2])
                            continue
                        ahead = n + 1 < len(order) and not (s <= cut < order[n + 1][0])
                        for m in range(ready, n + 1 + ahead):
                            prepare(*order[m][1])
                        ready = n + 1 + ahead
                        n += 1
                        if what == "average":
                            average(a[0], a[2])
                        else:
                            if keep_step:
                                dve.wait_ge(root_kept, STEPS * (1 if q == MEAN1 else 3) + (s if q == MEAN1 else a[2]) + 1)
                            add(*a)
                    if s == low_at:
                        low_of_unit(unit(q, 1), 1)
                    if s == 12 and more:
                        low_of_unit(unit(q + 1, 0), 0)
                    if s == cut:
                        add_spilled(*spilled)
                        ready = prepare_next()
                    if after:
                        after(s)

            def add_spilled(layer, g):
                n = dve.value_load(spill_n[0:1, 0:1], min_val=0, max_val=SPILL)

                def shift_and_sum(i, key):
                    dve.wait_ge(spill_shifted[layer], i * (NB + 1) + key + 1)
                    dve.tensor_scalar(one_hot[:, 0, 0, :], column[:], spill_gid[:], None,
                                      ALU.is_equal).then_inc(spill_hot[layer], 1)
                    dve.wait_ge(spill_hot[layer], i * NB + key + 1)
                    dve.tensor_scalar(spill_gid[:], spill_gid[:], float(-P), None, ALU.add)\
                        .then_inc(spill_shifted[layer], 1)
                    dve.wait_ge(spill_summed[layer], i * NB + key + 1)

                with dve.If(n > 0):
                    dve.wait_ge(tile_used, NSPLIT + RT * g)
                    added(g - 1, T - 1)
                    dve.nop().then_inc(spill_added[layer], 1)
                    dve.wait_ge(root_kept, STEPS * (1 + 2 * layer) + SPILL_STEP[layer] + 1)
                    dve.wait_ge(transposed, 2 * T * (2 + 2 * layer))
                    with dve.Fori(0, n) as i:
                        dve.tensor_copy(spill_gid[:], edges[:, bass.ds(i + MAIN, 1), 1])\
                            .then_inc(spill_shifted[layer], 1)
                        dve.wait_ge(spill_high[layer], i + 1)
                        dve.tensor_tensor(g_low[:, 0, :], raw[:, 0, :], g_high[:, 0, :].bitcast(f32),
                                          ALU.subtract).then_inc(spill_low[layer], 1)
                        for t in range(T):
                            shift_and_sum(i, t)
                            dve.tensor_scalar(x_rows[:, 0, :].rearrange("p (c n) -> p c n", c=2),
                                              agg[:, 0, :, 0:HALF], inv_count[:, t:t + 1], None, ALU.mult)\
                                .then_inc(spill_averaged[layer], 1)
                            dve.wait_ge(spill_turned_high[layer], i * T + t + 1)
                            dve.tensor_tensor(g_low[:, 1, :].rearrange("p (c n) -> p c n", c=2),
                                              prod[:, 0:2, 0:HALF],
                                              g_high[:, 1, :].rearrange("p (c n) -> p c n", c=2).bitcast(f32),
                                              ALU.subtract).then_inc(spill_turned_low[layer], 1)
                            dve.wait_ge(spill_multiplied[layer], i * T + t + 1)
                            a = acc[:, t, :].rearrange("p (c n) -> p c n", c=2)
                            dve.tensor_tensor(a, prod[:, 2:4, 0:HALF], a, ALU.add).then_inc(spill_added[layer], 1)
                            if t < T - 1:
                                dve.wait_ge(spill_added[layer], i * NB + t + 2)
                        with dve.Fori(1, R) as r:
                            for t in range(T):
                                shift_and_sum(i, r * T + t)
                                a = acc[:, t, :].rearrange("p (c n) -> p c n", c=2)
                                dve.scalar_tensor_tensor(a, agg[:, 0, :, 0:HALF],
                                                         inv_count[:, bass.ds(r * T + t, 1)], a,
                                                         ALU.mult, ALU.add).then_inc(spill_added[layer], 1)
                                dve.wait_ge(spill_added[layer], i * NB + r * T + t + 2)
                dve.end_ifs()

            dst_flat = dst_local[:].rearrange("p r i -> p (r i)")

            dve.wait_ge(consts_set, 1)
            link(dve.tensor_copy(column[:], column_i[:]))
            dve.tensor_copy(bucket_base[:], bucket_gid[:])
            dve.memset(go_on[:], 1.0)

            low_of_unit(0)
            for t in range(4):
                low_of_turn(0, t)
            turns = iter(range(4, T))
            turns_after = iter((1, 2) * T)

            F = [edge_f[:, n, :] for n in range(12)]
            TILE, DL, TYPE, SRC, KEY, ROW, GID, MPOS, CAP, FLAG, RANK, SPOS = F
            INT = [edge_i[:, n, :] for n in range(4)]
            dve.wait_ge(keys_loaded, 48)
            dve.tensor_scalar(INT[3], INT[0], LOG_P, None, ALU.arith_shift_right)
            dve.tensor_scalar(position[:], INT[0], P - 1, None, ALU.bitwise_and)
            dve.tensor_copy(TYPE, INT[1])
            link(dve.tensor_copy(SRC, INT[2]))
            dve.tensor_copy(TILE, INT[3])
            link(dve.tensor_copy(DL, position[:]))
            dve.tensor_copy(dl_bf[:], DL)
            dve.memset(go_on[:, :, 0], 0.0)
            dve.tensor_copy(small_bf[:, 0, :], column[:, 0:NB])
            link(dve.scalar_tensor_tensor(KEY, TYPE, float(T), TILE, ALU.mult, ALU.add))
            link(dve.tensor_copy(key_bf[:], KEY))
            for b in range(0, NB, SEG):
                link(dve.tensor_tensor(is_key[:, b:b + SEG, :], key_bf[:].unsqueeze(1).to_broadcast([EP, SEG, EJ]),
                                       small_bf[0:EP, 0, b:b + SEG].unsqueeze(2).to_broadcast([EP, SEG, EJ]),
                                       ALU.is_equal))
                for t in islice(turns, next(turns_after)):
                    low_of_turn(0, t)
                link(dve.tensor_reduce(small[0:EP, 0, b:b + SEG], is_key[:, b:b + SEG, :], axis=AX.X, op=ALU.add))
                for t in islice(turns, next(turns_after)):
                    low_of_turn(0, t)
            dve.tensor_copy(small_bf[0:EP, 1, :], small[0:EP, 0, :]).then_inc(rows_counted, 1)

            dve.wait_ge(rows_summed, 1)
            link(dve.tensor_scalar(small[0:EP, 1, :], agg[0:EP, 1, 0, 0:NB], -1.0, None, ALU.add))
            for b in range(0, NB, SEG):
                link(dve.tensor_tensor_scan(ranks[:].rearrange("p b j -> p (b j)"),
                                            go_on[:].rearrange("p b j -> p (b j)"),
                                            is_key[:, b:b + SEG, :].rearrange("p b j -> p (b j)"),
                                            0.0, ALU.mult, ALU.add))
                for c in range(SEG):
                    ins = dve.scalar_tensor_tensor(ranks[:, c, :], ranks[:, c, :], small[0:EP, 1, b + c:b + c + 1],
                                                   is_key[:, b + c, :], ALU.add, ALU.mult)
                link(ins)
                link(dve.tensor_reduce(RANK if b == 0 else FLAG, ranks[:].rearrange("p b j -> p j b"),
                                       axis=AX.X, op=ALU.add))
                if b:
                    link(dve.tensor_tensor(RANK, RANK, FLAG, ALU.add))

            dve.tensor_scalar(CAP, TILE, float(T - 1), float(-P * (BT - BT_LAST)), ALU.is_equal, ALU.mult)
            dve.scalar_tensor_tensor(ROW, TYPE, float(N), SRC, ALU.mult, ALU.add)
            dve.scalar_tensor_tensor(GID, KEY, float(P), DL, ALU.mult, ALU.add)
            link(dve.tensor_scalar(MPOS, TYPE, float(RT * P), None, ALU.mult))
            link(dve.scalar_tensor_tensor(MPOS, TILE, float(BT * P), MPOS, ALU.mult, ALU.add))
            dve.tensor_copy(payload[:, :, 0], ROW)
            dve.tensor_copy(payload[:, :, 1], GID)
            link(dve.tensor_tensor(MPOS, MPOS, RANK, ALU.add))
            link(dve.scalar_tensor_tensor(FLAG, RANK, float(-BT * P), CAP, ALU.add, ALU.is_ge))
            link(dve.tensor_tensor_scan(SPOS, FLAG, FLAG, 0.0, ALU.add, ALU.max))
            dve.tensor_copy(small_bf[0:EP, 2, 0:1], SPOS[:, EJ - 1:EJ]).then_inc(flags_counted, 1)
            dve.wait_ge(flags_summed, 1)
            dve.tensor_scalar(small[0:EP, 2, 0:1], agg[0:EP, 1, 0, 0:1], float(MAIN * P - 1), None, ALU.add)
            link(dve.tensor_scalar(small[:, 3, 0:1], agg[:, 1, 1, 0:1], float(P - 1), None, ALU.add))
            link(dve.tensor_copy(spill_n[:], small[:, 3, 0:1]))
            link(dve.tensor_scalar(spill_n[:], spill_n[:], LOG_P, None, ALU.arith_shift_right))
            link(dve.scalar_tensor_tensor(SPOS, SPOS, small[0:EP, 2, 0:1], MPOS, ALU.add, ALU.subtract))
            link(dve.tensor_tensor(SPOS, SPOS, FLAG, ALU.mult))
            link(dve.tensor_tensor(SPOS, SPOS, MPOS, ALU.add))
            link(dve.tensor_copy(INT[3], SPOS))
            dve.tensor_scalar(INT[0], INT[3], P - 1, None, ALU.bitwise_and)
            link(dve.tensor_scalar(INT[1], INT[3], LOG_P, None, ALU.arith_shift_right))
            dve.tensor_copy(TILE, INT[0])
            link(dve.tensor_copy(DL, INT[1]))
            link(dve.scalar_tensor_tensor(SPOS, TILE, float(COLS), DL, ALU.mult, ALU.add))
            link(dve.tensor_copy(position[:], SPOS))
            dve.nop().then_inc(positions_ready, 1)

            for u in range(NEAR, unit(ROOT1, 1)):
                low_of_unit(u)

            dve.wait_ge(transposed, 2 * T)
            dve.wait_ge(bias_loaded, 32)

            def one_hot_chunk(c):
                if c >= 2:
                    dve.wait_ge(chunk_counted, c - 1)
                dve.tensor_tensor(dst_hot[:, c % 2], column[0:EP, :].unsqueeze(1).to_broadcast([EP, CJ, P]),
                                  dl_bf[:, c * CJ:(c + 1) * CJ].unsqueeze(2).to_broadcast([EP, CJ, P]),
                                  ALU.is_equal).then_inc(hot_ready, 1)

            one_hot_chunk(0)
            for s in range(STEPS):
                if s + 1 < CHUNKS:
                    one_hot_chunk(s + 1)
                keep(STEPS * ROOT1 + s, s % T, s // T, s % BANKS, plus="bias")
                if s == 2:
                    low_of_unit(unit(ROOT1, 1))
                if s == 12:
                    low_of_unit(unit(ROOT1 + 1, 0))
                if s == CHUNKS:
                    dve.wait_ge(chunk_counted, CHUNKS)
                    link(dve.tensor_scalar(inv_count[:], agg[:, 0, 0, 0:NB], 1.0, None, ALU.max))
                    link(dve.reciprocal(inv_count[:], inv_count[:]))
                    dve.nop().then_inc(bucket_added, 2)
                    dve.nop().then_inc(low_ready, NRAW)
            dve.wait_ge(table_loaded, 16)
            used = dst_local[:, :, 0:RT]
            link(dve.tensor_copy(used, edges[:, 0:MAIN, 1].rearrange("p (r i) -> p r i", r=R)))
            link(dve.tensor_tensor(used, used, bucket_base[:, :, 0:RT], ALU.subtract))

            with dve.Fori(ROOT1 + 1, R - 1) as q:
                matrix(q, two_relations(2 * q - 2 * ROOT1 - 2, 2 * q - 2 * ROOT1 - 1))
            matrix(R - 1, averaging(R - 4, R - 3, 1), low_at=7)

            def keep_mean1(s):
                dve.wait_ge(bucket_added, 2 + T * (R - 2) + (s - T + 1 if s >= T else 0))
                keep(STEPS * MEAN1 + s, s % T, s // T, banks(2, True)(s), plus="acc")

            matrix(MEAN1, completing, keep_mean1, spilled=(0, R - 1))

            for s in range(STEPS):
                if s == 0:
                    low_of_turn(2, T - 1)
                    dve.wait_ge(transposed, 6 * T)
                    dve.wait_ge(h_stored, 16 * T)
                keep(STEPS * ROOT2 + s, s % T, s // T, banks(2)(s), plus=None)
                if s == 2:
                    low_of_unit(unit(ROOT2, 1))
                if s == 12:
                    low_of_unit(unit(ROOT2 + 1, 0))

            dve.wait_ge(root_kept, 3 * STEPS)
            for t in range(T):
                dve.wait_ge(x_biased, t + 1)
                dve.tensor_tensor(acc[:, t, :], acc[:, t, :], x_rows[:, t % 2, :], ALU.add)\
                    .then_inc(residual_added, 1)
                if t == 1:
                    low_of_unit(unit(ROOT2 + 1, 1))
                if t == 6:
                    low_of_unit(unit(ROOT2 + 2, 0))
            dve.wait_ge(residual_added, T)
            with dve.Fori(2, R - 1) as r:
                matrix(r + ROOT2, one_relation(r + R - 2, r - 1), low_at=5)
            matrix(MEAN2 - 1, averaging(2 * R - 3, R - 2, 3), low_at=7)

            def norm(t):
                dve.wait_ge(std_ready, t + 1)
                link(dve.reciprocal(std[:, t % 2, 1:2], std[:, t % 2, 0:1]))
                dve.tensor_scalar(acc[:, t, :], acc[:, t, :], moments[:, t % 2, 0:1], std[:, t % 2, 1:2],
                                  ALU.subtract, ALU.mult).then_inc(normed, 1)

            def keep_mean2(s):
                dve.wait_ge(bucket_added, 2 + T * (2 * R - 1) + (s - T + 1 if s >= T else 0))
                keep(STEPS * MEAN2 + s, s % T, s // T, banks(2)(s), plus="acc")

            def layer_norm(s):
                t = s - T
                if t >= 0:
                    dve.wait_ge(root_kept, 3 * STEPS + s + 1)
                    dve.bn_stats(stats[:, t % 2, 0, :], acc[:, t, 0:HALF])
                    link(dve.bn_stats(stats[:, t % 2, 1, :], acc[:, t, HALF:D]))
                    dve.bn_aggr(moments[:, t % 2, :], stats[:, t % 2].rearrange("p c s -> p (c s)"))\
                        .then_inc(var_ready, 1)
                if t >= 1:
                    norm(t - 1)

            matrix(MEAN2, finishing, keep_mean2, more=False, spilled=(1, 2 * R - 1), after=layer_norm, low_at=1)
            norm(T - 1)


def kernel(x, src, dst, edge_type_8, L0_gnn_W1, L0_gnn_root1, L0_gnn_b1, L0_gnn_W2, L0_gnn_root2, L0_gnn_b2):
    import numpy as np
    import concourse.bacc as bacc
    from concourse.bass_utils import run_bass_kernel_spmd

    W1, W2 = np.asarray(L0_gnn_W1), np.asarray(L0_gnn_W2)
    half = W1.shape[0] // 2
    w_all = np.concatenate([W1[1:half + 1], np.asarray(L0_gnn_root1)[None], W1[half + 1:], W1[:1],
                            np.asarray(L0_gnn_root2)[None], W2[1:], W2[:1]])
    arrays = {"x": x, "src": src, "dst": dst, "etype": edge_type_8, "w_all": w_all, "b1": L0_gnn_b1, "b2": L0_gnn_b2}
    arrays = {f"in_{k}": np.ascontiguousarray(v) for k, v in arrays.items()}
    nc = bacc.Bacc("TRN2", target_bir_lowering=False, num_devices=1)
    args = [nc.dram_tensor(k, v.shape, mybir.dt.from_np(v.dtype), kind="ExternalInput").ap()
            for k, v in arrays.items()]
    out = nc.dram_tensor("out", x.shape, mybir.dt.float32, kind="ExternalOutput").ap()
    rgcn_residual_layernorm(nc, *args, out)
    r = run_bass_kernel_spmd(nc, [arrays], core_ids=[0])
    return r.results[0]["out"]
```
